# Optimizing a Trainium2 kernel written in Bass

```python
import numpy as np
import jax
import jax.numpy as jnp

def _softmax(x, axis=-1):
    return jax.nn.softmax(x, axis=axis)

def _gelu(x):
    return jax.nn.gelu(x, approximate=True)

def _silu(x):
    return jax.nn.silu(x)

def _sigmoid(x):
    return jax.nn.sigmoid(x)

def _layernorm(x, axis=-1, eps=1e-05):
    m = jnp.mean(x, axis=axis, keepdims=True)
    v = jnp.var(x, axis=axis, keepdims=True)
    return (x - m) / jnp.sqrt(v + eps)

def _scatter_add(tgt, idx, src, axis=0):
    return tgt.at[idx].add(src)

def _segment_sum(src, seg, n):
    return jax.ops.segment_sum(src, seg, n)
kernel_name = 'mk_gps_d1_gnn_r8_107363'

def setup_inputs(seed: int=0):
    np.random.seed(seed)
    _w = jnp.asarray

    def _rec_inputs():
        import jax
        import jax.numpy as jnp
        _gk = jax.random.key(seed)
        x = -0.0002117 + 1 * jax.random.normal(jax.random.fold_in(_gk, 1), (6250, 256), jnp.float32)
        _s = jax.random.randint(jax.random.fold_in(_gk, 2), (50000,), 0, 6250, jnp.int32)
        _d = jax.random.randint(jax.random.fold_in(_gk, 3), (50000,), 0, 6250, jnp.int32)
        _loop = jnp.arange(6250, dtype=jnp.int32)
        src = jnp.concatenate([_s, _d, _loop])
        dst = jnp.concatenate([_d, _s, _loop])
        _o = jnp.argsort(dst, stable=True)
        src = src[_o]
        dst = dst[_o]
        edge_type_11 = jax.random.randint(jax.random.fold_in(_gk, 12), (106250,), 0, 11, jnp.int32)
        return (x, src, dst, edge_type_11)
    x, src, dst, edge_type_11 = _rec_inputs()

    def _L0_gnn_setup():
        import jax, jax.numpy as jnp
        import numpy as np
        N = 12500
        E = 400000
        D_IN = 256
        D_OUT = 256
        NUM_REL = 10
        key = jax.random.key(seed)
        k1, k2, k3, k4, k5, k6 = jax.random.split(key, 6)
        x = jax.random.normal(k1, (N, D_IN), dtype=jnp.float32)
        edge_index = jax.random.randint(k2, (2, E), 0, N, dtype=jnp.int64)
        rel = jax.random.randint(k3, (E,), 0, NUM_REL + 1, dtype=jnp.int64)
        stdv = 1.0 / np.sqrt(D_OUT)
        weight = jax.random.uniform(k4, (D_IN, D_OUT), dtype=jnp.float32, minval=-stdv, maxval=stdv)
        bias = jax.random.uniform(k5, (D_OUT,), dtype=jnp.float32, minval=-stdv, maxval=stdv)
        alpha = jax.random.normal(k6, (NUM_REL + 1, 1), dtype=jnp.float32)
        alpha = alpha.at[0].set(0.0)
        return {'x': x, 'edge_index': edge_index, 'rel': rel, 'weight': weight, 'bias': bias, 'alpha': alpha}
    _L0_gnn_all = _L0_gnn_setup()
    _L0_gnn_in = {k: v for k, v in _L0_gnn_all.items() if k in ('weight', 'bias', 'alpha')}
    del _L0_gnn_all

    def _L0_mix_setup():
        import jax, jax.numpy as jnp
        import numpy as np
        HEADS = 8
        DIM_HEAD = 32
        SCALE = DIM_HEAD ** (-0.5)
        EPS = 1e-05

        def _layernorm_gamma(x, gamma):
            mu = jnp.mean(x, axis=-1, keepdims=True)
            var = jnp.var(x, axis=-1, keepdims=True)
            return (x - mu) * jax.lax.rsqrt(var + EPS) * gamma
        key = jax.random.key(seed)
        k1, k2, k3 = jax.random.split(key, 3)
        B, N, D = (8, 2048, 256)
        hidden = HEADS * DIM_HEAD
        x = jax.random.normal(k1, (B, N, D), dtype=jnp.float32)
        Wqkv = jax.random.normal(k2, (D, 3 * hidden), dtype=jnp.float32) * D ** (-0.5)
        Wout = jax.random.normal(k3, (hidden, D), dtype=jnp.float32) * hidden ** (-0.5)
        gamma = jnp.ones((D,), dtype=jnp.float32)
        return {'x': x, 'Wqkv': Wqkv, 'Wout': Wout, 'gamma': gamma}
    _L0_mix_all = _L0_mix_setup()
    _L0_mix_in = {k: v for k, v in _L0_mix_all.items() if k in ('Wqkv', 'Wout', 'gamma')}
    del _L0_mix_all

    def _L0_ffn_setup():
        import jax, jax.numpy as jnp
        import numpy as np
        B, A = (512, 8)
        IN, OUT = (256, 256)
        SH1, SH2 = (256, 128)
        EH1, EH2 = (128, 64)
        E, TOPK = (4, 2)

        def _shared_mlp(x, W1, b1, W2, b2, W3, b3):
            h = jax.nn.relu(x @ W1 + b1)
            h = jax.nn.relu(h @ W2 + b2)
            return h @ W3 + b3

        def _experts_mlp(x, eW1, eb1, eW2, eb2, eW3, eb3):
            h = jax.nn.relu(jnp.einsum('baf,efh->ebah', x, eW1) + eb1[:, None, None, :])
            h = jax.nn.relu(jnp.einsum('ebah,ehg->ebag', h, eW2) + eb2[:, None, None, :])
            o = jnp.einsum('ebag,ego->ebao', h, eW3) + eb3[:, None, None, :]
            return jnp.moveaxis(o, 0, -1)
        key = jax.random.key(seed)
        ks = jax.random.split(key, 16)
        s = 0.05
        return {'x': jax.random.normal(ks[0], (B, A, IN), jnp.float32), 'sW1': jax.random.normal(ks[1], (IN, SH1), jnp.float32) * s, 'sb1': jnp.zeros((SH1,), jnp.float32), 'sW2': jax.random.normal(ks[2], (SH1, SH2), jnp.float32) * s, 'sb2': jnp.zeros((SH2,), jnp.float32), 'sW3': jax.random.normal(ks[3], (SH2, OUT), jnp.float32) * s, 'sb3': jnp.zeros((OUT,), jnp.float32), 'eW1': jax.random.normal(ks[4], (E, IN, EH1), jnp.float32) * s, 'eb1': jnp.zeros((E, EH1), jnp.float32), 'eW2': jax.random.normal(ks[5], (E, EH1, EH2), jnp.float32) * s, 'eb2': jnp.zeros((E, EH2), jnp.float32), 'eW3': jax.random.normal(ks[6], (E, EH2, OUT), jnp.float32) * s, 'eb3': jnp.zeros((E, OUT), jnp.float32), 'gW': jax.random.normal(ks[7], (IN, E), jnp.float32) * s, 'gb': jnp.zeros((E,), jnp.float32)}
    _L0_ffn_all = _L0_ffn_setup()
    _L0_ffn_in = {k: v for k, v in _L0_ffn_all.items() if k in ('sW1', 'sb1', 'sW2', 'sb2', 'sW3', 'sb3', 'eW1', 'eb1', 'eW2', 'eb2', 'eW3', 'eb3', 'gW', 'gb')}
    del _L0_ffn_all
    return {'x': x, 'src': src, 'dst': dst, 'edge_type_11': edge_type_11, 'L0_gnn_weight': _L0_gnn_in['weight'], 'L0_gnn_bias': _L0_gnn_in['bias'], 'L0_gnn_alpha': _L0_gnn_in['alpha'], 'L0_mix_Wqkv': _L0_mix_in['Wqkv'], 'L0_mix_Wout': _L0_mix_in['Wout'], 'L0_mix_gamma': _L0_mix_in['gamma'], 'L0_ffn_sW1': _L0_ffn_in['sW1'], 'L0_ffn_sb1': _L0_ffn_in['sb1'], 'L0_ffn_sW2': _L0_ffn_in['sW2'], 'L0_ffn_sb2': _L0_ffn_in['sb2'], 'L0_ffn_sW3': _L0_ffn_in['sW3'], 'L0_ffn_sb3': _L0_ffn_in['sb3'], 'L0_ffn_eW1': _L0_ffn_in['eW1'], 'L0_ffn_eb1': _L0_ffn_in['eb1'], 'L0_ffn_eW2': _L0_ffn_in['eW2'], 'L0_ffn_eb2': _L0_ffn_in['eb2'], 'L0_ffn_eW3': _L0_ffn_in['eW3'], 'L0_ffn_eb3': _L0_ffn_in['eb3'], 'L0_ffn_gW': _L0_ffn_in['gW'], 'L0_ffn_gb': _L0_ffn_in['gb']}

def reference(x, src, dst, edge_type_11, L0_gnn_weight, L0_gnn_bias, L0_gnn_alpha, L0_mix_Wqkv, L0_mix_Wout, L0_mix_gamma, L0_ffn_sW1, L0_ffn_sb1, L0_ffn_sW2, L0_ffn_sb2, L0_ffn_sW3, L0_ffn_sb3, L0_ffn_eW1, L0_ffn_eb1, L0_ffn_eW2, L0_ffn_eb2, L0_ffn_eW3, L0_ffn_eb3, L0_ffn_gW, L0_ffn_gb):
    import jax
    import jax.numpy as jnp

    def _L0_gnn_ref(x, edge_index, rel, weight, bias, alpha):
        import jax, jax.numpy as jnp
        import numpy as np
        N = 12500
        E = 400000
        D_IN = 256
        D_OUT = 256
        NUM_REL = 10
        w = alpha[rel, 0]
        support = x @ weight
        row, col = (edge_index[0], edge_index[1])
        out = jax.ops.segment_sum(w[:, None] * support[col], row, num_segments=x.shape[0])
        out = out + jax.ops.segment_sum(w[:, None] * support[row], col, num_segments=x.shape[0])
        return out + bias

    def _L0_mix_ref(x, Wqkv, Wout, gamma):
        import jax, jax.numpy as jnp
        import numpy as np
        HEADS = 8
        DIM_HEAD = 32
        SCALE = DIM_HEAD ** (-0.5)
        EPS = 1e-05

        def _layernorm_gamma(x, gamma):
            mu = jnp.mean(x, axis=-1, keepdims=True)
            var = jnp.var(x, axis=-1, keepdims=True)
            return (x - mu) * jax.lax.rsqrt(var + EPS) * gamma
        B, N, D = x.shape
        qkv = x @ Wqkv
        q, k, v = jnp.split(qkv, 3, axis=-1)

        def to_heads(t):
            return t.reshape(B, N, HEADS, DIM_HEAD).transpose(0, 2, 1, 3)
        q, k, v = map(to_heads, (q, k, v))
        q = jax.nn.softmax(q, axis=-1) * SCALE
        k = jax.nn.softmax(k, axis=2)
        context = jnp.einsum('bhnd,bhne->bhde', k, v)
        out = jnp.einsum('bhde,bhnd->bhne', context, q)
        out = out.transpose(0, 2, 1, 3).reshape(B, N, HEADS * DIM_HEAD)
        out = out @ Wout
        return _layernorm_gamma(out, gamma)

    def _L0_ffn_ref(x, sW1, sb1, sW2, sb2, sW3, sb3, eW1, eb1, eW2, eb2, eW3, eb3, gW, gb):
        import jax, jax.numpy as jnp
        import numpy as np
        B, A = (512, 8)
        IN, OUT = (256, 256)
        SH1, SH2 = (256, 128)
        EH1, EH2 = (128, 64)
        E, TOPK = (4, 2)

        def _shared_mlp(x, W1, b1, W2, b2, W3, b3):
            h = jax.nn.relu(x @ W1 + b1)
            h = jax.nn.relu(h @ W2 + b2)
            return h @ W3 + b3

        def _experts_mlp(x, eW1, eb1, eW2, eb2, eW3, eb3):
            h = jax.nn.relu(jnp.einsum('baf,efh->ebah', x, eW1) + eb1[:, None, None, :])
            h = jax.nn.relu(jnp.einsum('ebah,ehg->ebag', h, eW2) + eb2[:, None, None, :])
            o = jnp.einsum('ebag,ego->ebao', h, eW3) + eb3[:, None, None, :]
            return jnp.moveaxis(o, 0, -1)
        all_out = _experts_mlp(x, eW1, eb1, eW2, eb2, eW3, eb3)
        shared = _shared_mlp(x, sW1, sb1, sW2, sb2, sW3, sb3)
        gates = jax.nn.softmax(x @ gW + gb, axis=-1)
        topv, topi = jax.lax.top_k(gates, TOPK)
        topw = jax.nn.softmax(topv, axis=-1)
        sel = jnp.take_along_axis(all_out, topi[:, :, None, :], axis=-1)
        gated = jnp.sum(sel * topw[:, :, None, :], axis=-1)
        return shared + gated
    edge_index = jnp.stack([src, dst])
    xn = _layernorm(x, axis=-1)
    x = x + _L0_gnn_ref(xn, edge_index, edge_type_11, L0_gnn_weight, L0_gnn_bias, L0_gnn_alpha) + _L0_mix_ref(xn[None], L0_mix_Wqkv, L0_mix_Wout, L0_mix_gamma)[0]
    x = x + _L0_ffn_ref(_layernorm(x, axis=-1)[None], L0_ffn_sW1, L0_ffn_sb1, L0_ffn_sW2, L0_ffn_sb2, L0_ffn_sW3, L0_ffn_sb3, L0_ffn_eW1, L0_ffn_eb1, L0_ffn_eW2, L0_ffn_eb2, L0_ffn_eW3, L0_ffn_eb3, L0_ffn_gW, L0_ffn_gb)[0]
    return x

_drawn_inputs = setup_inputs


def setup_inputs(seed=0):
    import zlib

    import numpy as np

    out = dict(_drawn_inputs(seed))
    spreads = {'L0_mix_gamma': (1.0, 0.2),
     'L0_ffn_sb1': (0.0, 2.0),
     'L0_ffn_sb2': (0.0, 0.725),
     'L0_ffn_sb3': (0.0, 0.328),
     'L0_ffn_eb1': (0.0, 0.8),
     'L0_ffn_eb2': (0.0, 0.8),
     'L0_ffn_eb3': (0.0, 0.46),
     'L0_ffn_gb': (0.0, 0.8)}
    factors = {'L0_gnn_bias': 6.066,
     'L0_ffn_eW1': 5.046,
     'L0_ffn_eW2': 4.402,
     'L0_ffn_eW3': 3.552,
     'L0_ffn_gW': 3.363}
    for name, (base, spread) in spreads.items():
        noise = np.random.default_rng([zlib.crc32(name.encode()), seed]).standard_normal(out[name].shape)
        drawn = base * np.exp(spread * noise) if base else spread * noise
        out[name] = jnp.asarray(drawn.astype(out[name].dtype))
    for name, factor in factors.items():
        out[name] = (out[name] * factor).astype(out[name].dtype)
    return out
```

```python
from contextlib import ExitStack

import concourse.bass as bass
from concourse import mybir

F32 = mybir.dt.float32
I32 = mybir.dt.int32
ALU = mybir.AluOpType
ACT = mybir.ActivationFunctionType
AX = mybir.AxisListType

P = 128
EPS = 1e-5
HEADS = 8
COL_SHIFT, ROW_SHIFT, ID_BITS, REL_MASK = 4, 17, 13, 15
ID_MASK = (1 << ID_BITS) - 1
BIAS = 1 << 30
PAD_ROW = 8000


class Tally:

    def __init__(self, eng, sem):
        self.eng, self.sem, self.count = eng, sem, 0

    def mark(self, ins):
        ins.then_inc(self.sem, 1)
        self.count = self.count + 1

    def settle(self):
        self.eng.wait_ge(self.sem, self.count)


def repeat(eng, tally, body, times):
    start = tally.count if tally else 0
    body(0, False)
    per = tally.count - start if tally else 0
    with eng.Fori(1, times) as i:
        if per:
            tally.count = i * per + start
        body(i, True)
    if tally:
        tally.count = start + per * times


def program(nc, x, src, dst, edge_type, gnn_w, gnn_b, alpha, wqkv, wout, gamma,
            sw1, sb1, sw2, sb2, sw3, sb3, ew1, eb1, ew2, eb2, ew3, eb3, gw, gb, out):
    N, D = x.shape
    E = src.shape[0]
    R = alpha.shape[0]
    K2 = D // P
    U = 125
    UNITS = N // U
    PAIRS = UNITS // 2
    DH = D // HEADS
    SCALE = float(DH) ** -0.5
    NE, EH1, EH2 = ew1.shape[0], ew1.shape[2], ew2.shape[2]
    assert N % (2 * U) == 0 and D == 256 and E % U == 0 and N < PAD_ROW < 1 << ID_BITS
    ECOLS = E // U
    NCOLS = N // U
    MSGS = 2 * E + N
    BITS = (MSGS - 1).bit_length()
    COLS = (1 << BITS) // P
    BLOCKS = COLS // P
    TILES = -(-MSGS // P)
    RING = 16
    HALF = RING // 2
    LAG = 4
    BODIES = -(-TILES // RING)
    WIDE = N + P
    GT0 = D + U

    with ExitStack() as ctx:
        def sb(name, shape, dt=F32):
            return ctx.enter_context(nc.sbuf_tensor(name, shape, dt))

        def sem(name):
            return ctx.enter_context(nc.semaphore(name))

        ctx.enter_context(nc.allow_non_contiguous_dma(reason="bias columns of a few hundred elements"))

        xn_dram = nc.dram_tensor("xn_dram", (N, D), F32).ap()
        xnt_dram = nc.dram_tensor("xnt_dram", (P, K2, N), F32).ap()
        base_dram = nc.dram_tensor("base_dram", (N, D), F32).ap()

        bank = [ctx.enter_context(nc.psum_tensor(f"bank{i}", [P, 512], F32)) for i in range(8)]

        wqkv_s = sb("wqkv_s", [P, K2, 3 * D])
        wout_s = sb("wout_s", [P, K2, D])
        gnnw_s = sb("gnnw_s", [P, K2, D])
        sw1_s = sb("sw1_s", [P, K2, D])
        sw2_s = sb("sw2_s", [P, K2, P])
        sw3_s = sb("sw3_s", [P, D])
        ew1_s = sb("ew1_s", [P, K2, NE, EH1])
        ew2_s = sb("ew2_s", [P, NE, EH2])
        ew3_s = sb("ew3_s", [P, NE // 2, D])
        gw_s = sb("gw_s", [P, K2, NE])
        sb1_s = sb("sb1_s", [P, K2])
        sb2_s = sb("sb2_s", [P, 1])
        eb1_s = sb("eb1_s", [P, NE])
        eb2_s = sb("eb2_s", [P, NE // 2])
        b5_s = sb("b5_s", [NE + 1, D])
        gamma_b = sb("gamma_b", [P, D])
        gnnb_b = sb("gnnb_b", [P, D])
        gb_b = sb("gb_b", [P, NE])
        alpha_b = sb("alpha_b", [P, R])
        ident = sb("ident", [P, P])
        ones = sb("ones", [P, P])
        zeros = sb("zeros", [1, P])
        iota_p = sb("iota_p", [P, 1], I32)
        bit_i = sb("bit_i", [P, 7], I32)
        sign = sb("sign", [P, 7])
        before = sb("before", [P, NE, NE])
        expert_i = sb("expert_i", [NE, 2, 2, EH2], I32)
        spread = sb("spread", [NE, NE // 2, P])
        carrier = sb("carrier", [P, 1])
        half_pow = sb("half_pow", [P, 1])
        nodes = sb("nodes", [P, WIDE])

        xin = sb("xin", [P, 2, D])
        xnt = sb("xnt", [P, 2, K2, U])
        t0 = sb("t0", [P, 2, D])
        t1 = sb("t1", [P, 2, D])
        t2 = sb("t2", [P, 2, D])
        stats = sb("stats", [P, 2, 6])
        mv = sb("mv", [P, 2, 2])
        rstd = sb("rstd", [P, 2, 1])
        head = sb("head", [P, 2, 2, HEADS])
        kmax = sb("kmax", [P, K2, U])
        nkmax = sb("nkmax", [P, K2])
        nkrow = sb("nkrow", [1, K2, P])
        ctx_t = sb("ctx_t", [P, K2, P])
        ksum_r = sb("ksum_r", [P, K2])
        mix_w = sb("mix_w", [P, K2, D])
        h1t = sb("h1t", [P, 2, K2, U])
        h2t = sb("h2t", [P, 2, U])
        t3t = sb("t3t", [P, 2, K2, U])
        e1t = sb("e1t", [P, 2, NE, U])
        e2t = sb("e2t", [P, 2, NE // 2, U])
        e2g = sb("e2g", [P, 2, NE // 2, U])
        g5 = sb("g5", [P, 2, NE + 1])
        g5t = sb("g5t", [NE + 1, 2, U])
        gs = sb("gs", [P, 2, 8, NE])
        gsq = sb("gsq", [P, 2, 3, NE, NE])

        sort_a = sb("sort_a", [P, COLS])
        sort_b = sb("sort_b", [P, COLS])
        agg = sb("agg", [P, K2, WIDE])
        gath = sb("gath", [P, RING, D])
        hot = sb("hot", [P, RING, P])
        src_s = agg[:, 0, 0:ECOLS].bitcast(I32)
        dst_s = agg[:, 0, ECOLS:2 * ECOLS].bitcast(I32)
        typ_s = agg[:, 0, 2 * ECOLS:3 * ECOLS].bitcast(I32)
        mid_s = agg[:, 0, 3 * ECOLS:4 * ECOLS].bitcast(I32)
        node_s = agg[:, 0, 4 * ECOLS:4 * ECOLS + NCOLS].bitcast(I32)
        row_f = sb("row_f", [P, COLS])
        wgt = sb("wgt", [P, COLS])
        first = sb("first", [1, COLS], I32)
        cols = sb("cols", [P, RING], I32)

        s_w = sem("weights_loaded")
        s_e = sem("edges_loaded")
        s_const = sem("constants_made")
        s_constv = sem("constants_made_dve")
        s_v = sem("dve_order")
        s_pl = sem("pool_order")
        s_xl = [sem(f"x_loaded{s}") for s in range(2)]
        s_tl = [sem(f"xt_loaded{s}") for s in range(2)]
        s_stored = [sem(f"stored{s}") for s in range(2)]
        s_tstored = [sem(f"t_stored{s}") for s in range(2)]

        n_var, n_rstd, n_xn, n_tr, n_trc, n_kt, n_kmax = (sem(n) for n in (
            "n_var", "n_rstd", "n_xn", "n_transposed", "n_xnt", "n_kt", "n_kmax"))
        m_neg, m_row, m_rowc = (sem(n) for n in ("neg_kmax", "neg_kmax_row", "neg_kmax_row_copied"))
        c_kv, c_exp, c_v, c_ctx, c_end = (sem(n) for n in ("c_kv", "c_kexp", "c_v", "c_context", "c_context_ended"))
        w_ctx, w_mm, w_done = (sem(n) for n in ("w_context_copied", "w_product", "mix_w_ready"))
        q_q, q_sub, q_exp, q_norm, q_tr, q_trc, q_o, q_var, q_rstd, q_ln, q_base = (sem(n) for n in (
            "q_q", "q_shifted", "q_exp", "q_softmax", "q_transposed", "q_t", "q_mix", "q_var", "q_rstd",
            "q_layernorm", "q_base"))
        s_turn, s_eva, s_key = sem("sort_blocks_turned"), sem("sort_blocks_copied"), sem("sort_turn_wanted")
        g_idx, g_mm, g_hot, g_acc = (sem(n) for n in ("columns_ready", "tile_summed", "one_hot", "accumulated"))
        g_in = [sem(f"gathered{j}") for j in range(RING)]
        f_ag, f_y, f_var, f_rstd, f_zn, f_tr, f_znt, f_h, f_relu, f_2, f_h2, f_e2, f_log, f_gl, f_ge = (
            sem(n) for n in ("f_agg", "f_y", "f_var", "f_rstd", "f_zn", "f_turned", "f_znt", "f_layer1",
                             "f_relu1", "f_layer2", "f_relu2s", "f_relu2e", "f_logits", "f_gatelogits", "f_gateexp"))
        f_p, f_pe, f_g, f_gt, f_gtc, f_gb, f_e2g, f_o, f_res = (sem(n) for n in (
            "f_gates", "f_gatesexp", "f_weights", "f_weights_turned", "f_weights_t", "f_spread", "f_gated",
            "f_out", "f_result"))

        turns, at_, plain = [], 0, [[(512 * q, 512 * q + 512, 1.0)] for q in range(4)]
        for k in range(8, BITS + 1):
            at_ = 1 - at_
            turns.append((at_, plain))
            at_ = (at_ + k - 7 + 1) % 2
            if k < 14:
                signs = [[(512 * q, 512 * q + 512, sign[:, k - 7:k - 6])] for q in range(4)]
            elif k < BITS:
                signs = [[(P * c, P * c + P, -1.0 if c >> (k - 14) & 1 else 1.0) for c in range(4 * q, 4 * q + 4)]
                         for q in range(4)]
            else:
                signs = plain
            turns.append((at_, signs))
            at_ = (at_ + 7) % 2
        turns.append((1 - at_, plain))

        block = ctx.enter_context(nc.Block())
        NW = 20

        @block.sync
        def _(sp):
            for to, fro in ((src_s, src), (dst_s, dst), (typ_s, edge_type)):
                sp.dma_start(to[0:U], fro.rearrange("(p n) -> p n", p=U)).then_inc(s_e, 16)
            loads = [
                (wqkv_s[:], wqkv.rearrange("(k p) n -> p k n", p=P)),
                (wout_s[:], wout.rearrange("(k p) n -> p k n", p=P)),
                (gnnw_s[:], gnn_w.rearrange("(k p) n -> p k n", p=P)),
                (sw1_s[:], sw1.rearrange("(k p) n -> p k n", p=P)),
                (sw2_s[:], sw2.rearrange("(k p) n -> p k n", p=P)),
                (sw3_s[:], sw3),
                (ew1_s[:, 0], ew1[:, 0:P].rearrange("e p h -> p e h")),
                (ew1_s[:, 1], ew1[:, P:2 * P].rearrange("e p h -> p e h")),
                (ew2_s[:], ew2.rearrange("e p h -> p e h")),
                (ew3_s[:], ew3.rearrange("(q h) g o -> (h g) q o", h=2)),
                (gw_s[:], gw.rearrange("(k p) n -> p k n", p=P)),
                (sb1_s[:], sb1.rearrange("(k p) -> p k", p=P)),
                (sb2_s[:], sb2.rearrange("(p a) -> p a", a=1)),
                (eb1_s[:], eb1.rearrange("e p -> p e")),
                (eb2_s[:], eb2.rearrange("(q h) g -> (h g) q", h=2)),
                (b5_s[0:NE], eb3),
                (b5_s[NE:NE + 1], sb3.rearrange("(a d) -> a d", a=1)),
                (gamma_b[:], gamma.rearrange("(a d) -> a d", a=1).to_broadcast([P, D])),
                (gnnb_b[:], gnn_b.rearrange("(a d) -> a d", a=1).to_broadcast([P, D])),
                (alpha_b[:], alpha.rearrange("r a -> a r").to_broadcast([P, R])),
                (gb_b[:], gb.rearrange("(a d) -> a d", a=1).to_broadcast([P, NE])),
            ]
            assert len(loads) == NW + 1
            for to, fro in loads:
                sp.dma_start(to, fro).then_inc(s_w, 16)

            def rows_of(u):
                return u * U if isinstance(u, int) else sp.snap(u * U)

            def load_x(u, b, s, warm):
                at = rows_of(u)
                if warm:
                    sp.wait_ge(n_xn, u - 1)
                sp.dma_start(xin[0:U, s], x[bass.ds(at, U), :]).then_inc(s_xl[s], 16)

            def store_xn(u, s):
                at = rows_of(u)
                sp.wait_ge(n_xn, u + 1)
                sp.dma_start(xn_dram[bass.ds(at, U), :], t0[0:U, s]).then_inc(s_stored[s], 16)
                sp.wait_ge(s_w, 16)
                sp.wait_ge(n_trc, u + 1)
                sp.dma_start(xnt_dram[:, :, bass.ds(at, U)], xnt[:, s]).then_inc(s_tstored[s], 16)

            def p1(b, warm):
                for s in range(2):
                    load_x(2 * b + s, b, s, warm)
                for s in range(2):
                    store_xn(2 * b + s, s)
            repeat(sp, None, p1, PAIRS)
            for s in range(2):
                sp.wait_ge(s_tstored[s], 16 * PAIRS)
            sp.wait_ge(n_kt, UNITS)
            sp.wait_ge(n_xn, UNITS)

            def p2(b, warm):
                for s in range(2):
                    at = rows_of(2 * b + s)
                    if warm:
                        sp.wait_ge(c_kv, 2 * b + s - 1)
                    sp.dma_start(xnt[:, s], xnt_dram[:, :, bass.ds(at, U)]).then_inc(s_tl[s], 16)
            repeat(sp, None, p2, PAIRS)
            sp.wait_ge(c_kv, UNITS)

            def p3(b, warm):
                for s in range(2):
                    u = 2 * b + s
                    at = rows_of(u)
                    if warm:
                        sp.wait_ge(q_q, u - 1)
                    sp.dma_start(xnt[:, s], xnt_dram[:, :, bass.ds(at, U)]).then_inc(s_tl[s], 16)
                    if warm:
                        sp.wait_ge(q_base, u - 1)
                    sp.dma_start(xin[0:U, s], x[bass.ds(at, U), :]).then_inc(s_xl[s], 16)
                for s in range(2):
                    u = 2 * b + s
                    at = rows_of(u)
                    sp.wait_ge(q_base, u + 1)
                    sp.dma_start(base_dram[bass.ds(at, U), :], t2[0:U, s]).then_inc(s_stored[s], 16)
            repeat(sp, None, p3, PAIRS)
            for s in range(2):
                sp.wait_ge(s_stored[s], 32 * PAIRS)

            def p5(b, warm):
                for s in range(2):
                    u = 2 * b + s
                    at = rows_of(u)
                    if warm:
                        sp.wait_ge(f_res, u - 1)
                    sp.dma_start(xin[0:U, s], base_dram[bass.ds(at, U), :]).then_inc(s_xl[s], 16)
                for s in range(2):
                    u = 2 * b + s
                    at = rows_of(u)
                    sp.wait_ge(f_res, u + 1)
                    sp.dma_start(out[bass.ds(at, U), :], t2[0:U, s]).then_inc(s_stored[s], 16)
            repeat(sp, None, p5, PAIRS)
            for s in range(2):
                sp.wait_ge(s_stored[s], 48 * PAIRS)

        @block.gpsimd
        def _(pool):
            t = Tally(pool, s_pl)
            t.mark(pool.memset(ident[:], 0.0))
            t.mark(pool.memset(ones[:], 1.0))
            t.mark(pool.memset(half_pow[:], -0.5))
            pool.memset(zeros[:], 0.0).then_inc(s_const, 1)
            t.mark(pool.memset(g5[:], 1.0))
            t.mark(pool.memset(before[:], 1.0))
            t.settle()
            pool.affine_select(out=ident[:], in_=ident[:], compare_op=ALU.not_equal, fill=1.0, base=0,
                               pattern=[[-1, P]], channel_multiplier=1).then_inc(s_const, 1)
            pool.affine_select(out=before[:], in_=before[:], compare_op=ALU.is_gt, fill=0.0, base=0,
                               pattern=[[1, NE], [-1, NE]], channel_multiplier=0).then_inc(s_const, 1)
            pool.iota(iota_p[:], [[0, 1]], base=0, channel_multiplier=1).then_inc(s_const, 1)
            pool.iota(expert_i[:], [[2, 2], [1, 2], [0, EH2]], base=0, channel_multiplier=-1).then_inc(s_const, 1)
            pool.iota(nodes[:], [[1, WIDE]], base=0, channel_multiplier=0,
                      allow_small_or_imprecise_dtypes=True).then_inc(s_const, 1)
            pool.iota(node_s[0:U], [[1, NCOLS]], base=0, channel_multiplier=NCOLS).then_inc(s_const, 1)

            def inverse_std(ready, done):
                def body(b, warm):
                    for s in range(2):
                        pool.wait_ge(ready, 2 * b + s + 1)
                        pool.tensor_tensor(rstd[0:U, s], mv[0:U, s, 1:2], half_pow[0:U], ALU.pow).then_inc(done, 1)
                return body
            repeat(pool, None, inverse_std(n_var, n_rstd), PAIRS)

            def p3(b, warm):
                for s in range(2):
                    u = 2 * b + s
                    pool.wait_ge(q_var, u + 1)
                    pool.tensor_tensor(rstd[0:U, s], mv[0:U, s, 1:2], half_pow[0:U], ALU.pow).then_inc(q_rstd, 1)
                    pool.wait_ge(q_ln, u + 1)
                    t.mark(pool.tensor_tensor(t1[0:U, s], t1[0:U, s], gamma_b[0:U], ALU.mult))
                    pool.wait_ge(s_xl[s], 16 * (PAIRS + 1) + 16 * b)
                    if warm:
                        pool.wait_ge(s_stored[s], 16 * PAIRS + 16 * b)
                    else:
                        pool.wait_ge(s_w, 16 * (NW + 1))
                    t.mark(pool.tensor_tensor(t2[0:U, s], xin[0:U, s], gnnb_b[0:U], ALU.add))
                    t.settle()
                    pool.tensor_tensor(t2[0:U, s], t2[0:U, s], t1[0:U, s], ALU.add).then_inc(q_base, 1)
            repeat(pool, t, p3, PAIRS)

            for s in range(2):
                pool.wait_ge(s_stored[s], 16 * PAIRS)

            def gathers(i, warm):
                for j in range(RING):
                    if j % HALF == 0:
                        t.settle()
                        pool.wait_ge(g_idx, 2 * i + j // HALF + 1)
                        t.mark(pool.tensor_tensor(carrier[0:1], half_pow[0:1], half_pow[0:1], ALU.add))
                    pool.indirect_dma_start(gath[:, j], None, xn_dram[:, :],
                                            bass.IndirectOffsetOnAxis(ap=cols[:, j:j + 1], axis=0)).then_inc(g_in[j], 16)
            repeat(pool, t, gathers, BODIES)
            repeat(pool, None, inverse_std(f_var, f_rstd), PAIRS)

        @block.scalar
        def _(act):
            act.wait_ge(s_const, 7)
            act.wait_ge(s_w, 16 * (NW + 1))

            def p1(b, warm):
                for s in range(2):
                    u = 2 * b + s
                    act.wait_ge(n_tr, u + 1)
                    if warm:
                        act.wait_ge(s_tstored[s], 16 * b)
                        act.wait_ge(n_kt, u - 1)
                    act.copy(xnt[:, s], bank[s][:, 0:K2 * U].rearrange("p (k n) -> p k n", k=K2)).then_inc(n_trc, 1)
            repeat(act, None, p1, PAIRS)
            for s in range(2):
                act.wait_ge(s_stored[s], 16 * PAIRS)
            act.wait_ge(m_row, 1)
            act.copy(nkrow[:], bank[4][0:1, 0:D].rearrange("p (k n) -> p k n", k=K2)).then_inc(m_rowc, 1)

            def p2(b, warm):
                for s in range(2):
                    u = 2 * b + s
                    act.wait_ge(c_kv, u + 1)
                    if warm:
                        act.wait_ge(c_ctx, u - 1)
                    act.activation(t0[0:U, s], bank[s][0:U, 0:D], ACT.Exp).then_inc(c_exp, 1)
            repeat(act, None, p2, PAIRS)

            def p3(b, warm):
                for s in range(2):
                    u = 2 * b + s
                    act.wait_ge(q_sub, u + 1)
                    act.activation(t0[0:U, s], t0[0:U, s], ACT.Exp).then_inc(q_exp, 1)
                    act.wait_ge(q_tr, u + 1)
                    if warm:
                        act.wait_ge(q_o, u - 1)
                    act.copy(h1t[:, s], bank[2 + s][:, 0:K2 * U].rearrange("p (k n) -> p k n", k=K2)).then_inc(q_trc, 1)
            repeat(act, None, p3, PAIRS)

            for n, (to, signs) in enumerate(turns):
                for q in range(2):
                    act.wait_ge(s_turn, 4 * n + q + 1)
                    for lo, hi, sc in signs[q]:
                        last = act.activation((sort_a, sort_b)[to][:, lo:hi], bank[q][:, lo - 512 * q:hi - 512 * q],
                                              ACT.Copy, scale=sc)
                    last.then_inc(s_eva, 1)

            def p5(b, warm):
                for s in range(2):
                    u = 2 * b + s
                    if warm:
                        act.wait_ge(f_y, u - 1)
                    else:
                        act.wait_ge(g_acc, RING * BODIES)
                    act.copy(xnt[:, s], agg[:, :, bass.ds(u * U, U)]).then_inc(f_ag, 1)
                    act.wait_ge(f_tr, u + 1)
                    if warm:
                        act.wait_ge(f_h, u - 1)
                    act.copy(t3t[:, s], bank[s][:, D:D + K2 * U].rearrange("p (k n) -> p k n", k=K2)).then_inc(f_znt, 1)
                    act.wait_ge(f_gl, u + 1)
                    act.activation(gs[0:U, s, 1], gs[0:U, s, 0], ACT.Exp).then_inc(f_ge, 1)
                    act.wait_ge(f_h, u + 1)
                    if warm:
                        act.wait_ge(f_2, u - 1)
                    for k in range(K2):
                        act.activation(h1t[:, s, k], bank[2 + s][:, k * U:k * U + U], ACT.Relu,
                                       bias=sb1_s[:, k:k + 1])
                    for e in range(NE):
                        last = act.activation(e1t[:, s, e], bank[4 + s][:, e * U:e * U + U], ACT.Relu,
                                              bias=eb1_s[:, e:e + 1])
                    last.then_inc(f_relu, 1)
                    act.wait_ge(f_p, u + 1)
                    act.activation(gs[0:U, s, 4], gs[0:U, s, 3], ACT.Exp).then_inc(f_pe, 1)
                    act.wait_ge(f_2, u + 1)
                    if warm:
                        act.wait_ge(f_o, u - 1)
                    act.activation(h2t[:, s], bank[2 + s][:, D:D + U], ACT.Relu, bias=sb2_s[:, 0:1]).then_inc(f_h2, 1)
                    act.wait_ge(f_gt, u + 1)
                    act.copy(g5t[:, s], bank[2 + s][0:NE + 1, GT0:GT0 + U]).then_inc(f_gtc, 1)
            repeat(act, None, p5, PAIRS)

        @block.vector
        def _(dve):
            t = Tally(dve, s_v)

            def do(ins):
                t.mark(ins)
                t.settle()

            V = nc.vector
            dve.wait_ge(s_const, 7)
            dve.wait_ge(s_w, 16 * (NW + 1))
            for b in range(7):
                t.mark(V.tensor_scalar(bit_i[:, b:b + 1], iota_p[:], b, 1, ALU.logical_shift_right, ALU.bitwise_and))
            t.mark(V.memset(kmax[:], -3.0e38))
            t.mark(V.tensor_scalar(spread[:].rearrange("e q p -> e (q p)"),
                                   expert_i[:].rearrange("e q h g -> e (q h g)"), 0.0, None, ALU.is_equal))
            t.settle()
            do(V.tensor_scalar(sign[:], bit_i[:], -2.0, 1.0, ALU.mult, ALU.add))
            V.memset(ctx_t[:], 0.0).then_inc(s_constv, 1)

            def normalise(src_ap, s, stat_sem, rstd_sem, u, to, done, warm_free=None):
                t.mark(V.bn_stats(stats[0:U, s], src_ap))
                t.settle()
                t.mark(V.memset(carrier[96:97], 0.0))
                do(V.bn_aggr(mv[0:U, s], stats[0:U, s]))
                V.tensor_scalar(mv[0:U, s, 1:2], mv[0:U, s, 1:2], EPS, None, ALU.add).then_inc(stat_sem, 1)
                dve.wait_ge(rstd_sem, u + 1)
                if warm_free:
                    warm_free()
                V.tensor_scalar(to, src_ap, mv[0:U, s, 0:1], rstd[0:U, s], ALU.subtract, ALU.mult).then_inc(done, 1)

            def p1(b, warm):
                for s in range(2):
                    u = 2 * b + s
                    dve.wait_ge(s_xl[s], 16 * b + 16)

                    def free():
                        if warm:
                            dve.wait_ge(s_stored[s], 16 * b)
                            dve.wait_ge(n_tr, u - 1)
                    normalise(xin[0:U, s], s, n_var, n_rstd, u, t0[0:U, s], n_xn, free)
                for s in range(2):
                    u = 2 * b + s
                    dve.wait_ge(n_kt, u + 1)
                    dve.wait_ge(n_kmax, u)
                    V.tensor_tensor(kmax[:], bank[2 + s][:, 0:K2 * U].rearrange("p (k n) -> p k n", k=K2), kmax[:],
                                    ALU.max).then_inc(n_kmax, 1)
            repeat(dve, t, p1, PAIRS)
            dve.wait_ge(n_kmax, UNITS)
            do(V.tensor_reduce(nkmax[:], kmax[:], AX.X, ALU.max))
            V.tensor_scalar(nkmax[:], nkmax[:], -1.0, None, ALU.mult).then_inc(m_neg, 1)

            def p2(b, warm):
                for s in range(2):
                    u = 2 * b + s
                    dve.wait_ge(c_kv, u + 1)
                    if warm:
                        dve.wait_ge(c_ctx, u - 1)
                    V.tensor_copy(t1[0:U, s], bank[2 + s][0:U, 0:D]).then_inc(c_v, 1)
            repeat(dve, t, p2, PAIRS)

            dve.wait_ge(c_end, K2)
            for h in range(HEADS):
                k, p0 = h // 4, DH * (h % 4)
                t.mark(V.tensor_copy(ctx_t[p0:p0 + DH, k, p0:p0 + DH], bank[4 + k][p0:p0 + DH, h * DH:(h + 1) * DH]))
            for k in range(K2):
                t.mark(V.reciprocal(ksum_r[:, k:k + 1], bank[6 + k][:, 0:1]))
            t.settle()
            V.tensor_scalar(ksum_r[:], ksum_r[:], SCALE, None, ALU.mult).then_inc(w_ctx, 1)
            dve.wait_ge(w_ctx, 1)
            dve.wait_ge(w_mm, 1)
            for k in range(K2):
                V.tensor_scalar(mix_w[:, k], bank[2][:, k * D:k * D + D], ksum_r[:, k:k + 1], None,
                                ALU.mult).then_inc(w_done, 1)

            def p3(b, warm):
                for s in range(2):
                    u = 2 * b + s
                    q = bank[s][0:U, 0:D].rearrange("p (h d) -> p h d", h=HEADS)
                    e = t0[0:U, s].rearrange("p (h d) -> p h d", h=HEADS)
                    dve.wait_ge(q_q, u + 1)
                    do(V.tensor_reduce(head[0:U, s, 0], q, AX.X, ALU.max))
                    if warm:
                        dve.wait_ge(q_tr, u - 1)
                    V.tensor_tensor(e, q, head[0:U, s, 0].unsqueeze(2).to_broadcast([U, HEADS, DH]),
                                    ALU.subtract).then_inc(q_sub, 1)
                for s in range(2):
                    u = 2 * b + s
                    e = t0[0:U, s].rearrange("p (h d) -> p h d", h=HEADS)
                    dve.wait_ge(q_exp, u + 1)
                    do(V.tensor_reduce(head[0:U, s, 0], e, AX.X, ALU.add))
                    do(V.reciprocal(head[0:U, s, 1], head[0:U, s, 0]))
                    V.tensor_tensor(e, e, head[0:U, s, 1].unsqueeze(2).to_broadcast([U, HEADS, DH]),
                                    ALU.mult).then_inc(q_norm, 1)
                for s in range(2):
                    u = 2 * b + s
                    dve.wait_ge(q_o, u + 1)

                    def free():
                        if warm:
                            dve.wait_ge(q_base, u - 1)
                    normalise(bank[4 + s][0:U, 0:D], s, q_var, q_rstd, u, t1[0:U, s], q_ln, free)
            repeat(dve, t, p3, PAIRS)

            dve.wait_ge(s_e, 48)
            A, B = sort_a, sort_b
            Ai, Bi = A[:].bitcast(I32), B[:].bitcast(I32)
            pad = BIAS | PAD_ROW << ROW_SHIFT | R
            t.mark(V.memset(Ai, pad))
            do(V.tensor_scalar(typ_s[0:U], typ_s[0:U], BIAS, None, ALU.bitwise_or))
            for row, col, c0 in ((src_s, dst_s, 0), (dst_s, src_s, ECOLS)):
                do(V.tensor_scalar(mid_s[0:U], col[0:U], COL_SHIFT, None, ALU.logical_shift_left))
                do(V.tensor_tensor(mid_s[0:U], mid_s[0:U], typ_s[0:U], ALU.bitwise_or))
                do(V.tensor_scalar(Ai[0:U, c0:c0 + ECOLS], row[0:U], ROW_SHIFT, None, ALU.logical_shift_left))
                do(V.tensor_tensor(Ai[0:U, c0:c0 + ECOLS], Ai[0:U, c0:c0 + ECOLS], mid_s[0:U], ALU.bitwise_or))
            own = Ai[0:U, 2 * ECOLS:2 * ECOLS + NCOLS]
            do(V.tensor_scalar(own, node_s[0:U], ROW_SHIFT, BIAS | R, ALU.logical_shift_left, ALU.bitwise_or))
            do(V.tensor_scalar(node_s[0:U], node_s[0:U], COL_SHIFT, None, ALU.logical_shift_left))
            do(V.tensor_tensor(own, own, node_s[0:U], ALU.bitwise_or))
            do(V.tensor_scalar(A[:], A[:], sign[:, 0:1], None, ALU.mult))

            buf = [A, B]
            at = 0
            nready = 0

            def compare(j, k, negated=False, ready=False):
                nonlocal at, nready
                todo = []

                def pick(y, x0, x1, op):
                    todo.append((y, x0, x1, op))
                a, o = buf[at], buf[1 - at]
                i = 1 << j
                if k is None:
                    va, vo = (z[:].rearrange("p (o t i) -> p o t i", t=2, i=i) for z in (a, o))
                    pick(vo[:, :, 0], va[:, :, 0], va[:, :, 1], ALU.min)
                    pick(vo[:, :, 1], va[:, :, 0], va[:, :, 1], ALU.max)
                else:
                    m = 1 << (k - j - 1)
                    va, vo = (z[:].rearrange("p (o d m t i) -> p o d m t i", d=2, m=m, t=2, i=i) for z in (a, o))
                    for d in range(2):
                        for lo in range(2):
                            op = ALU.min if lo == d else ALU.max
                            mid = 0 if m == 1 else slice(0, m)
                            pick(vo[:, :, d, mid, lo], va[:, :, d, mid, 0], va[:, :, d, mid, 1], op)
                for n, (y, x0, x1, op) in enumerate(todo):
                    if negated:
                        ins = V.scalar_tensor_tensor(y, x1, -1.0, x0, ALU.mult, op)
                    else:
                        ins = V.tensor_tensor(y, x0, x1, op)
                    if ready and n == len(todo) - 1:
                        ins.then_inc(s_key, 1)
                        nready += 1
                        dve.wait_ge(s_key, nready)
                    else:
                        t.mark(ins)
                t.settle()
                at = 1 - at

            nturn = 0

            def turn():
                nonlocal at, nturn
                signs = turns[nturn][1]
                for q in range(2, 4):
                    dve.wait_ge(s_turn, 4 * nturn + q + 1)
                    for lo, hi, sc in signs[q]:
                        t.mark(V.tensor_scalar(buf[1 - at][:, lo:hi], bank[q][:, lo - 512 * q:hi - 512 * q], sc, None,
                                               ALU.mult))
                t.settle()
                nturn += 1
                dve.wait_ge(s_eva, 2 * nturn)
                at = 1 - at

            for k in range(1, 8):
                for j in range(k - 1, -1, -1):
                    compare(j, k if k < 7 else None, ready=(k == 7 and j == 0))
            for k in range(8, BITS + 1):
                turn()
                for j in range(k - 1, 6, -1):
                    compare(j - 7, None if k == BITS else k - 7, negated=(j == k - 1), ready=(j == 7))
                turn()
                for j in range(6, -1, -1):
                    compare(j, None, ready=(j == 0))
            turn()
            assert nturn == len(turns)
            S, T = buf[at], buf[1 - at]
            Si, Ti = S[:].bitcast(I32), T[:].bitcast(I32)

            do(V.tensor_scalar(Ti, Si, ROW_SHIFT, ID_MASK, ALU.logical_shift_right, ALU.bitwise_and))
            t.mark(V.tensor_copy(row_f[:], Ti))
            do(V.tensor_scalar(first[:], Ti[0:1], float(N - 1), None, ALU.min))
            do(V.tensor_scalar(Ti, Si, REL_MASK, None, ALU.bitwise_and))
            tmp = agg[:, 1, 0:COLS]
            for r in range(R):
                if r == 0:
                    do(V.tensor_scalar(wgt[:], Ti, 0.0, alpha_b[:, 0:1], ALU.is_equal, ALU.mult))
                else:
                    do(V.tensor_scalar(tmp, Ti, float(r), alpha_b[:, r:r + 1], ALU.is_equal, ALU.mult))
                    do(V.tensor_tensor(wgt[:], wgt[:], tmp, ALU.add))
            do(V.memset(agg[:], 0.0))

            def unpack_cols(tile0, j0):
                V.tensor_scalar(cols[:, j0:j0 + HALF], Si[:, bass.ds(tile0, HALF)], COL_SHIFT, ID_MASK,
                                ALU.logical_shift_right, ALU.bitwise_and).then_inc(g_idx, 1)
            unpack_cols(0, 0)
            unpack_cols(HALF, HALF)

            def accumulate(tile, j, r0):
                dve.wait_ge(g_mm, tile + 1)
                dve.wait_ge(g_acc, tile)
                window = agg[:, :, bass.ds(r0, P)]
                V.tensor_tensor(window, bank[j % 8][:, 0:K2 * P].rearrange("p (k n) -> p k n", k=K2), window,
                                ALU.add).then_inc(g_acc, 1)

            def firsts(tile, count):
                _, vals = nc.values_load_multi_w_load_instructions(
                    first[0:1, bass.ds(tile, count)], engines=[dve.engine], min_val=0, max_val=N - 1,
                    skip_runtime_bounds_check_because="clamped to the last node when unpacked, and rows are not negative")
                return vals

            def gather_body(i, warm):
                before_rows = firsts(RING * i - LAG, LAG) if warm else None
                for q in range(RING // LAG):
                    rows = firsts(RING * i + q * LAG, LAG)
                    for m in range(LAG):
                        j = q * LAG + m
                        tile = RING * i + j
                        V.tensor_scalar(hot[:, j], nodes[:, bass.ds(rows[m], P)], row_f[:, bass.ds(tile, 1)],
                                        wgt[:, bass.ds(tile, 1)], ALU.is_equal, ALU.mult).then_inc(g_hot, 1)
                        if before_rows:
                            accumulate(tile - LAG, (j - LAG) % RING, before_rows[m])
                    if q == 0 and warm:
                        unpack_cols(RING * i + HALF, HALF)
                    if q == 2:
                        unpack_cols(RING * i + RING, 0)
                    before_rows = rows

            repeat(dve, t, gather_body, BODIES)
            rows = firsts(RING * BODIES - LAG, LAG)
            for m in range(LAG):
                accumulate(RING * BODIES - LAG + m, RING - LAG + m, rows[m])

            def p5(b, warm):
                for s in range(2):
                    u = 2 * b + s
                    dve.wait_ge(f_y, u + 1)
                    dve.wait_ge(s_xl[s], 16 * (2 * PAIRS + 1) + 16 * b)
                    do(V.tensor_tensor(t1[0:U, s], bank[s][0:U, 0:D], xin[0:U, s], ALU.add))

                    def free():
                        if warm:
                            dve.wait_ge(f_tr, u - 1)
                    normalise(t1[0:U, s], s, f_var, f_rstd, u, t0[0:U, s], f_zn, free)
                    g = gs[0:U, s]
                    h = head[0:U, s, 0]
                    dve.wait_ge(f_log, u + 1)
                    do(V.tensor_tensor(g[:, 0], bank[s][0:U, 0:NE], gb_b[0:U], ALU.add))
                    do(V.tensor_reduce(h[:, 0:1], g[:, 0], AX.X, ALU.max))
                    V.tensor_scalar(g[:, 0], g[:, 0], h[:, 0:1], None, ALU.subtract).then_inc(f_gl, 1)
                    dve.wait_ge(f_ge, u + 1)
                    do(V.tensor_reduce(h[:, 0:1], g[:, 1], AX.X, ALU.add))
                    do(V.reciprocal(h[:, 1:2], h[:, 0:1]))
                    V.tensor_scalar(g[:, 3], g[:, 1], h[:, 1:2], None, ALU.mult).then_inc(f_p, 1)
                    dve.wait_ge(f_p, u + 1)
                    mine = g[:, 3].unsqueeze(2).to_broadcast([U, NE, NE])
                    other = g[:, 3].unsqueeze(1).to_broadcast([U, NE, NE])
                    sq = gsq[0:U, s]
                    t.mark(V.tensor_tensor(sq[:, 0], other, mine, ALU.is_gt))
                    do(V.tensor_tensor(sq[:, 1], other, mine, ALU.is_equal))
                    do(V.tensor_tensor(sq[:, 1], sq[:, 1], before[0:U], ALU.mult))
                    do(V.tensor_tensor(sq[:, 2], sq[:, 1], sq[:, 0], ALU.add))
                    do(V.tensor_reduce(g[:, 5], sq[:, 2], AX.X, ALU.add))
                    dve.wait_ge(f_pe, u + 1)
                    do(V.scalar_tensor_tensor(g[:, 6], g[:, 5], 1.5, g[:, 4], ALU.is_lt, ALU.mult))
                    do(V.tensor_reduce(h[:, 2:3], g[:, 6], AX.X, ALU.add))
                    do(V.reciprocal(h[:, 3:4], h[:, 2:3]))
                    if warm:
                        dve.wait_ge(f_gt, u - 1)
                    V.tensor_scalar(g5[0:U, s, 0:NE], g[:, 6], h[:, 3:4], None, ALU.mult).then_inc(f_g, 1)
                    dve.wait_ge(f_2, u + 1)
                    for q in range(NE // 2):
                        last = V.tensor_scalar(e2t[:, s, q], bank[6][:, q * U:q * U + U], eb2_s[:, q:q + 1], 0.0,
                                               ALU.add, ALU.max)
                    last.then_inc(f_e2, 1)
                    dve.wait_ge(f_gb, u + 1)
                    if warm:
                        dve.wait_ge(f_o, u - 1)
                    V.tensor_tensor(e2g[:, s], e2t[:, s], bank[6][:, D:D + 2 * U].rearrange("p (q n) -> p q n", q=2),
                                    ALU.mult).then_inc(f_e2g, 1)
                    dve.wait_ge(f_o, u + 1)
                    if warm:
                        dve.wait_ge(s_stored[s], 32 * PAIRS + 16 * b)
                    else:
                        dve.wait_ge(s_stored[s], 32 * PAIRS)
                    V.tensor_tensor(t2[0:U, s], bank[7][0:U, 0:D], t1[0:U, s], ALU.add).then_inc(f_res, 1)
            repeat(dve, t, p5, PAIRS)

        @block.tensor
        def _(pe):
            M = nc.tensor.matmul
            pe.wait_ge(s_const, 7)
            pe.wait_ge(s_w, 16 * (NW + 1))

            def turn_unit(src_ap, s, to, o, done):
                for k in range(K2):
                    last = pe.transpose(to[:, o + k * U:o + k * U + U], src_ap[:, k * P:(k + 1) * P], ident[0:U, 0:U])
                last.then_inc(done, 1)

            def p1(b, warm):
                for s in range(2):
                    u = 2 * b + s
                    pe.wait_ge(n_xn, u + 1)
                    if warm:
                        pe.wait_ge(n_trc, u - 1)
                    turn_unit(t0[0:U, s], s, bank[s], 0, n_tr)
                for s in range(2):
                    u = 2 * b + s
                    pe.wait_ge(n_trc, u + 1)
                    if warm:
                        pe.wait_ge(n_kmax, u - 1)
                    for f in range(K2):
                        for k in range(K2):
                            last = M(bank[2 + s][:, f * U:f * U + U], wqkv_s[:, k, D + f * P:D + f * P + P],
                                     xnt[:, s, k], start=(k == 0), stop=(k == K2 - 1))
                    last.then_inc(n_kt, 1)
            repeat(pe, None, p1, PAIRS)
            pe.wait_ge(m_neg, 1)
            for k in range(K2):
                last = pe.transpose(bank[4][0:1, k * P:(k + 1) * P], nkmax[:, k:k + 1], ident[:])
            last.then_inc(m_row, 1)
            pe.wait_ge(m_rowc, 1)

            def p2(b, warm):
                for s in range(2):
                    u = 2 * b + s
                    pe.wait_ge(s_tl[s], 16 * b + 16)
                    if warm:
                        pe.wait_ge(c_exp, u - 1)
                        pe.wait_ge(c_v, u - 1)
                    for k in range(K2):
                        M(bank[2 + s][0:U, 0:D], xnt[:, s, k], wqkv_s[:, k, 2 * D:3 * D], start=(k == 0),
                          stop=(k == K2 - 1))
                    for k in range(K2):
                        M(bank[s][0:U, 0:D], xnt[:, s, k], wqkv_s[:, k, D:2 * D], start=(k == 0), stop=False)
                    M(bank[s][0:U, 0:D], ones[0:1, 0:U], nkrow[:].rearrange("p k n -> p (k n)"), start=False,
                      stop=True).then_inc(c_kv, 1)
                for s in range(2):
                    u = 2 * b + s
                    pe.wait_ge(c_exp, u + 1)
                    pe.wait_ge(c_v, u + 1)
                    first_unit = not warm and s == 0
                    for k in range(K2):
                        M(bank[4 + k][:, 0:D], t1[0:U, s, k * P:(k + 1) * P], t0[0:U, s], start=first_unit, stop=False,
                          skip_group_check=True)
                    for k in range(K2):
                        last = M(bank[6 + k][:, 0:1], t0[0:U, s, k * P:(k + 1) * P], ones[0:U, 0:1],
                                 start=first_unit, stop=False, skip_group_check=True)
                    last.then_inc(c_ctx, 1)
            repeat(pe, None, p2, PAIRS)
            for k in range(K2):
                M(bank[4 + k][:, 0:D], zeros[:], b5_s[0:1], start=False, stop=True, skip_group_check=True)
                M(bank[6 + k][:, 0:1], zeros[:], ones[0:1, 0:1], start=False, stop=True,
                  skip_group_check=True).then_inc(c_end, 1)
            pe.wait_ge(w_ctx, 1)
            pe.wait_ge(s_constv, 1)
            for k in range(K2):
                last = M(bank[2][:, k * D:k * D + D], ctx_t[:, k], wout_s[:, k], start=True, stop=True)
            last.then_inc(w_mm, 1)
            pe.wait_ge(w_done, K2)

            def p3(b, warm):
                for s in range(2):
                    u = 2 * b + s
                    pe.wait_ge(s_tl[s], 16 * PAIRS + 16 * b + 16) if warm else pe.wait_ge(s_tl[s], 16 * PAIRS + 16)
                    if warm:
                        pe.wait_ge(q_sub, u - 1)
                    for k in range(K2):
                        last = M(bank[s][0:U, 0:D], xnt[:, s, k], wqkv_s[:, k, 0:D], start=(k == 0), stop=(k == K2 - 1))
                    last.then_inc(q_q, 1)
                for s in range(2):
                    u = 2 * b + s
                    pe.wait_ge(q_norm, u + 1)
                    if warm:
                        pe.wait_ge(q_trc, u - 1)
                    turn_unit(t0[0:U, s], s, bank[2 + s], 0, q_tr)
                for s in range(2):
                    u = 2 * b + s
                    pe.wait_ge(q_trc, u + 1)
                    if warm:
                        pe.wait_ge(q_ln, u - 1)
                    for k in range(K2):
                        last = M(bank[4 + s][0:U, 0:D], h1t[:, s, k], mix_w[:, k], start=(k == 0), stop=(k == K2 - 1))
                    last.then_inc(q_o, 1)
            repeat(pe, None, p3, PAIRS)
            pe.wait_ge(q_trc, UNITS)

            for n, (to, _) in enumerate(turns):
                pe.wait_ge(s_key, n + 1)
                for q in range(4):
                    for c in range(4 * q, 4 * q + 4):
                        last = pe.transpose(bank[q][:, (c - 4 * q) * P:(c - 4 * q + 1) * P],
                                            (sort_a, sort_b)[1 - to][:, c * P:(c + 1) * P], ident[:])
                    last.then_inc(s_turn, 1)

            def sums(i, warm):
                for j in range(RING):
                    tile = RING * i + j
                    pe.wait_ge(g_in[j], 16 * i + 16)
                    pe.wait_ge(g_hot, tile + 1)
                    if warm or j >= 8:
                        pe.wait_ge(g_acc, tile - 7)
                    elif j == 0:
                        pe.wait_ge(q_ln, UNITS)
                        pe.wait_ge(s_eva, 2 * len(turns))
                    for k in range(K2):
                        last = M(bank[j % 8][:, k * P:(k + 1) * P], gath[:, j, k * P:(k + 1) * P], hot[:, j],
                                 start=True, stop=True)
                    last.then_inc(g_mm, 1)
            repeat(pe, None, sums, BODIES)

            def p5(b, warm):
                for s in range(2):
                    u = 2 * b + s
                    pe.wait_ge(f_ag, u + 1)
                    if warm:
                        pe.wait_ge(f_gl, u - 1)
                    else:
                        pe.wait_ge(g_acc, RING * BODIES)
                    for k in range(K2):
                        last = M(bank[s][0:U, 0:D], xnt[:, s, k], gnnw_s[:, k], start=(k == 0), stop=(k == K2 - 1))
                    last.then_inc(f_y, 1)
                    pe.wait_ge(f_zn, u + 1)
                    turn_unit(t0[0:U, s], s, bank[s], D, f_tr)
                    pe.wait_ge(f_znt, u + 1)
                    if warm:
                        pe.wait_ge(f_gtc, u - 1)
                        pe.wait_ge(f_relu, u - 1)
                    for k in range(K2):
                        last = M(bank[s][0:U, 0:NE], t3t[:, s, k], gw_s[:, k], start=(k == 0),
                                 stop=(k == K2 - 1))
                    last.then_inc(f_log, 1)
                    for f in range(K2):
                        for k in range(K2):
                            M(bank[2 + s][:, f * U:f * U + U], sw1_s[:, k, f * P:f * P + P], t3t[:, s, k],
                              start=(k == 0), stop=(k == K2 - 1))
                    for e in range(NE):
                        for k in range(K2):
                            last = M(bank[4 + s][:, e * U:e * U + U], ew1_s[:, k, e], t3t[:, s, k], start=(k == 0),
                                     stop=(k == K2 - 1))
                    last.then_inc(f_h, 1)
                    pe.wait_ge(f_relu, u + 1)
                    for k in range(K2):
                        M(bank[2 + s][:, D:D + U], sw2_s[:, k], h1t[:, s, k], start=(k == 0), stop=(k == K2 - 1))
                    pe.wait_ge(f_e2g, u)
                    for e in range(NE):
                        p0 = EH2 * (e % 2)
                        last = M(bank[6][p0:p0 + EH2, (e // 2) * U:(e // 2) * U + U], ew2_s[:, e], e1t[:, s, e],
                                 start=True, stop=True)
                    last.then_inc(f_2, 1)
                    pe.wait_ge(f_g, u + 1)
                    pe.wait_ge(f_h2, u + 1)
                    pe.transpose(bank[2 + s][0:NE + 1, GT0:GT0 + U], g5[0:U, s], ident[0:U, 0:U]).then_inc(f_gt, 1)
                    pe.wait_ge(f_gtc, u + 1)
                    pe.wait_ge(f_e2, u + 1)
                    for q in range(NE // 2):
                        last = M(bank[6][:, D + q * U:D + q * U + U], spread[:, q], g5t[0:NE, s], start=True, stop=True)
                    last.then_inc(f_gb, 1)
                    pe.wait_ge(f_res, u)
                    M(bank[7][0:U, 0:D], h2t[:, s], sw3_s[:], start=True, stop=False)
                    M(bank[7][0:U, 0:D], g5t[:, s], b5_s[:], start=False, stop=False)
                    pe.wait_ge(f_e2g, u + 1)
                    for q in range(NE // 2):
                        last = M(bank[7][0:U, 0:D], e2g[:, s, q], ew3_s[:, q], start=False, stop=(q == 1))
                    last.then_inc(f_o, 1)
            repeat(pe, None, p5, PAIRS)


_INS = ["x", "src", "dst", "edge_type_11", "L0_gnn_weight", "L0_gnn_bias", "L0_gnn_alpha", "L0_mix_Wqkv",
        "L0_mix_Wout", "L0_mix_gamma", "L0_ffn_sW1", "L0_ffn_sb1", "L0_ffn_sW2", "L0_ffn_sb2", "L0_ffn_sW3",
        "L0_ffn_sb3", "L0_ffn_eW1", "L0_ffn_eb1", "L0_ffn_eW2", "L0_ffn_eb2", "L0_ffn_eW3", "L0_ffn_eb3",
        "L0_ffn_gW", "L0_ffn_gb"]


def kernel(**inputs):
    import numpy as _np
    import concourse.bacc as _bacc
    from concourse import mybir as _mybir
    from concourse.bass_utils import run_bass_kernel_spmd as _run

    nc = _bacc.Bacc("TRN2", target_bir_lowering=False, num_devices=1)
    arrays, args = {}, []
    for name in _INS:
        a = _np.ascontiguousarray(inputs[name])
        arrays[f"in_{name}_dram"] = a
        args.append(nc.dram_tensor(f"in_{name}_dram", a.shape, _mybir.dt.from_np(a.dtype), kind="ExternalInput").ap())
    shape = inputs["x"].shape
    args.append(nc.dram_tensor("out_0_dram", shape, _mybir.dt.float32, kind="ExternalOutput").ap())
    program(nc, *args)
    r = _run(nc, [arrays], core_ids=[0])
    return r.results[0]["out_0_dram"]
```

```python
from contextlib import ExitStack

import concourse.bass as bass
from concourse import mybir

F32 = mybir.dt.float32
I32 = mybir.dt.int32
ALU = mybir.AluOpType
ACT = mybir.ActivationFunctionType
AX = mybir.AxisListType

P = 128
EPS = 1e-5
HEADS = 8
COL_SHIFT, ROW_SHIFT, ID_BITS, REL_MASK = 4, 17, 13, 15
ID_MASK = (1 << ID_BITS) - 1
BIAS = 1 << 30
PAD_ROW = 8000


class Tally:

    def __init__(self, eng, sem):
        self.eng, self.sem, self.count, self.marks = eng, sem, 0, 0

    def mark(self, ins):
        ins.then_inc(self.sem, 1)
        self.count = self.count + 1
        self.marks += 1

    def settle(self):
        self.eng.wait_ge(self.sem, self.count)


class FinalUnits:

    def __init__(self, nc, eng, first_rows, ring, unit_rows, units):
        self.nc, self.eng, self.first_rows, self.ring = nc, eng, first_rows, ring
        self.unit_rows, self.units = unit_rows, units
        self.begun = eng.alloc_register(f"units_begun_{eng.engine.name}")
        eng.reg_mov(self.begun, 0)

    def next(self):
        return self.eng.snap(self.begun, min_val=0, max_val=self.units - 1)

    def left(self):
        return self.eng.If(self.eng.snap(self.begun, min_val=0, max_val=self.units) < self.units)

    def begin(self):
        self.eng.reg_add(self.begun, self.begun, 1)

    def due(self, i):
        _, rows = self.nc.values_load_multi_w_load_instructions(
            self.first_rows[0:1, bass.ds(i * self.ring, 1)], engines=[self.eng.engine], min_val=0,
            max_val=self.unit_rows * self.units - 1,
            skip_runtime_bounds_check_because="clamped to the last node when unpacked, and rows are not negative")
        n = self.eng.snap(self.begun, min_val=0, max_val=self.units)
        return self.eng.If(n * self.unit_rows + (self.unit_rows - 1) < rows[0])


def repeat(eng, tally, body, first, end):
    start = tally.count
    body(first, False)
    per = tally.count - start
    with eng.Fori(first + 1, end) as i:
        if per:
            tally.count = i * per + (start - first * per)
        body(i, True)
    tally.count = start + per * (end - first)


def program(nc, x, src, dst, edge_type, gnn_w, gnn_b, alpha, wqkv, wout, gamma,
            sw1, sb1, sw2, sb2, sw3, sb3, ew1, eb1, ew2, eb2, ew3, eb3, gw, gb, out):
    N, D = x.shape
    E = src.shape[0]
    R = alpha.shape[0]
    K2 = D // P
    U = 125
    UNITS = N // U
    PAIRS = UNITS // 2
    DH = D // HEADS
    SCALE = float(DH) ** -0.5
    NE, EH1, EH2 = ew1.shape[0], ew1.shape[2], ew2.shape[2]
    assert N % (2 * U) == 0 and D == 256 and E % U == 0 and N < PAD_ROW < 1 << ID_BITS
    ECOLS = E // U
    NCOLS = N // U
    MSGS = 2 * E + N
    BITS = (MSGS - 1).bit_length()
    COLS = (1 << BITS) // P
    BLOCKS = COLS // P
    TILES = -(-MSGS // P)
    RING = 16
    HALF = RING // 2
    SUMS = 4
    LAG = 4
    BODIES = -(-TILES // RING)
    WIDE = -(-(N + P) // D) * D
    CHUNK = 10
    CHUNKS = UNITS // CHUNK
    GROUP = CHUNK // 2
    assert UNITS % CHUNK == 0 and UNITS * D <= K2 * WIDE and 4 * PAIRS < BODIES
    GT0 = D + U

    with ExitStack() as ctx:
        def sb(name, shape, dt=F32):
            return ctx.enter_context(nc.sbuf_tensor(name, shape, dt))

        def sem(name):
            return ctx.enter_context(nc.semaphore(name))

        ctx.enter_context(nc.allow_non_contiguous_dma(reason="bias columns of a few hundred elements"))

        xn_dram = nc.dram_tensor("xn_dram", (N, D), F32).ap()
        xnt_dram = nc.dram_tensor("xnt_dram", (P, UNITS, K2 * U), F32).ap()
        xb_dram = nc.dram_tensor("xb_dram", (N, D), F32).ap()
        base_dram = nc.dram_tensor("base_dram", (N, D), F32).ap()

        bank = [ctx.enter_context(nc.psum_tensor(f"bank{i}", [P, 512], F32)) for i in range(8)]

        wqkv_s = sb("wqkv_s", [P, K2, 3 * D])
        wout_s = sb("wout_s", [P, K2, D])
        gnnw_s = sb("gnnw_s", [P, K2, D])
        sw1_s = sb("sw1_s", [P, K2, D])
        sw2_s = sb("sw2_s", [P, K2, P])
        sw3_s = sb("sw3_s", [P, D])
        ew1_s = sb("ew1_s", [P, K2, NE, EH1])
        ew2_s = sb("ew2_s", [P, NE, EH2])
        ew3_s = sb("ew3_s", [P, NE // 2, D])
        gw_s = sb("gw_s", [P, K2, NE])
        sb1_s = sb("sb1_s", [P, K2])
        sb2_s = sb("sb2_s", [P, 1])
        eb1_s = sb("eb1_s", [P, NE])
        eb2_s = sb("eb2_s", [P, NE // 2])
        b5_s = sb("b5_s", [NE + 1, D])
        gamma_b = sb("gamma_b", [P, D])
        gnnb_b = sb("gnnb_b", [P, D])
        gb_b = sb("gb_b", [P, NE])
        alpha_b = sb("alpha_b", [P, R])
        ident = sb("ident", [P, P])
        ones = sb("ones", [P, P])
        zeros = sb("zeros", [1, P])
        iota_p = sb("iota_p", [P, 1], I32)
        bit_i = sb("bit_i", [P, 7], I32)
        sign = sb("sign", [P, 7])
        before = sb("before", [P, NE, NE])
        expert_i = sb("expert_i", [NE, 2, 2, EH2], I32)
        spread = sb("spread", [NE, NE // 2, P])
        carrier = sb("carrier", [P, 1])
        newton = sb("newton", [P, 2])
        mdif = sb("mdif", [P, 2])
        half_pow = sb("half_pow", [P, 1])
        nodes = sb("nodes", [P, WIDE])

        xin = sb("xin", [P, 2, D])
        xnt = sb("xnt", [P, 2, K2, U])
        t0 = sb("t0", [P, 2, D])
        t1 = sb("t1", [P, 2, D])
        t2 = sb("t2", [P, 2, D])
        stats = sb("stats", [P, 2, 6])
        mv = sb("mv", [P, 2, 2])
        rstd = sb("rstd", [P, 2, 1])
        n_stat = sem("n_stats")
        head = sb("head", [P, 2, 3, HEADS])
        kmax = sb("kmax", [P, K2, U])
        nkmax = sb("nkmax", [P, K2])
        nkrow = sb("nkrow", [1, K2, P])
        ctx_t = sb("ctx_t", [P, K2, P])
        ksum_r = sb("ksum_r", [P, K2])
        mix_w = sb("mix_w", [P, K2, D])
        h1t = sb("h1t", [P, 2, K2, U])
        h2t = sb("h2t", [P, 2, U])
        t3t = sb("t3t", [P, 2, K2, U])
        e1t = sb("e1t", [P, 2, NE, U])
        e2t = sb("e2t", [P, 2, NE // 2, U])
        e2g = sb("e2g", [P, 2, NE // 2, U])
        g5 = sb("g5", [P, 2, NE + 1])
        g5t = sb("g5t", [NE + 1, 2, U])
        gs = sb("gs", [P, 2, 8, NE])
        gsq = sb("gsq", [P, 2, 3, NE, NE])

        sort_a = sb("sort_a", [P, COLS])
        sort_b = sb("sort_b", [P, COLS])
        agg = sb("agg", [P, K2, WIDE])
        gath = sb("gath", [P, RING, D])
        hot = sb("hot", [P, RING, P])
        src_s = sort_b[:, 0:ECOLS].bitcast(I32)
        dst_s = sort_b[:, ECOLS:2 * ECOLS].bitcast(I32)
        node_s = sort_b[:, 2 * ECOLS:2 * ECOLS + NCOLS].bitcast(I32)
        row_f = sb("row_f", [P, COLS])
        wgt = sb("wgt", [P, COLS])
        typ_s = row_f[:, 0:ECOLS].bitcast(I32)
        mid_s = row_f[:, ECOLS:2 * ECOLS].bitcast(I32)
        x_all = agg[:].rearrange("p k n -> p (k n)").rearrange("p (u d) -> p u d", d=D)
        gath_flat = gath[:].rearrange("p r d -> p (r d)")
        xnt_ring = gath_flat[:, 0:CHUNK * K2 * U].rearrange("p (m k n) -> p m k n", m=CHUNK, k=K2)
        stats_all = sb("stats_all", [P, UNITS, 6])
        mean_all = sb("mean_all", [P, UNITS])
        var_all = sb("var_all", [P, UNITS])
        dif_all = sb("dif_all", [P, UNITS])
        rstd_all = sb("rstd_all", [P, UNITS])
        first = sb("first", [1, COLS], I32)
        cols = sb("cols", [P, RING], I32)

        s_w = sem("weights_loaded")
        s_e = sem("edges_loaded")
        s_const = sem("constants_made")
        s_constv = sem("constants_made_dve")
        s_v = sem("dve_order")
        s_pl = sem("pool_order")
        s_xl = [sem(f"x_loaded{s}") for s in range(2)]
        s_tl = sem("xt_pair_loaded")
        s_stored = [sem(f"stored{s}") for s in range(2)]
        s_tstored = [sem(f"t_stored{s}") for s in range(2)]

        f_order = sem("final_order")
        s_x = [sem(f"x_loaded_chunk{c}") for c in range(CHUNKS)]
        n_var, n_rstd, n_xn, n_cp, n_tr, n_trc, n_kt, n_kmax, n_store, n_tstore0, n_tstore1, n_zero = (
            sem(n) for n in ("n_var", "n_rstd", "n_xn", "n_copied", "n_transposed", "n_xnt", "n_kt", "n_kmax",
                             "n_xn_stored", "n_xnt_stored0", "n_xnt_stored1", "n_agg_zeroed"))
        n_tstore = [n_tstore0, n_tstore1]
        b_ld = [sem(f"b_x_loaded{s}") for s in range(2)]
        b_st = [sem(f"b_xb_stored{s}") for s in range(2)]
        b_sum = sem("b_xb")
        s_order = {e: sem(f"{e}_order") for e in ("sp", "act", "pe")}
        m_neg, m_row, m_rowc = (sem(n) for n in ("neg_kmax", "neg_kmax_row", "neg_kmax_row_copied"))
        c_kv, c_exp, c_v, c_ctx, c_end = (sem(n) for n in ("c_kv", "c_kexp", "c_v", "c_context", "c_context_ended"))
        w_ctx, w_mm, w_done = (sem(n) for n in ("w_context_copied", "w_product", "mix_w_ready"))
        q_q, q_sub, q_exp, q_norm, q_tr, q_trc, q_o, q_var, q_rstd, q_ln, q_base = (sem(n) for n in (
            "q_q", "q_shifted", "q_exp", "q_softmax", "q_transposed", "q_t", "q_mix", "q_var", "q_rstd",
            "q_layernorm", "q_base"))
        s_turn, s_eva, s_key = sem("sort_blocks_turned"), sem("sort_blocks_copied"), sem("sort_turn_wanted")
        g_idx, g_mm, g_hot, g_acc = (sem(n) for n in ("columns_ready", "tile_summed", "one_hot", "accumulated"))
        g_in = [sem(f"gathered{j}") for j in range(RING)]
        f_ag, f_y, f_var, f_rstd, f_zn, f_tr, f_znt, f_h, f_relu, f_2, f_h2, f_e2, f_log, f_gl, f_ge = (
            sem(n) for n in ("f_agg", "f_y", "f_var", "f_rstd", "f_zn", "f_turned", "f_znt", "f_layer1",
                             "f_relu1", "f_layer2", "f_relu2s", "f_relu2e", "f_logits", "f_gatelogits", "f_gateexp"))
        f_p, f_pe, f_g, f_gt, f_gtc, f_gb, f_e2g, f_o, f_res = (sem(n) for n in (
            "f_gates", "f_gatesexp", "f_weights", "f_weights_turned", "f_weights_t", "f_spread", "f_gated",
            "f_out", "f_result"))

        turns, at_, plain = [], 0, [[(512 * q, 512 * q + 512, 1.0)] for q in range(4)]
        for k in range(8, BITS + 1):
            at_ = 1 - at_
            turns.append((at_, plain))
            at_ = (at_ + k - 7 + 1) % 2
            if k < 14:
                signs = [[(512 * q, 512 * q + 512, sign[:, k - 7:k - 6])] for q in range(4)]
            elif k < BITS:
                signs = [[(P * c, P * c + P, -1.0 if c >> (k - 14) & 1 else 1.0) for c in range(4 * q, 4 * q + 4)]
                         for q in range(4)]
            else:
                signs = plain
            turns.append((at_, signs))
            at_ = (at_ + 7) % 2
        turns.append((1 - at_, plain))

        block = ctx.enter_context(nc.Block())
        NW = 20

        @block.sync
        def _(sp):
            for to, fro in ((src_s, src), (dst_s, dst), (typ_s, edge_type)):
                sp.dma_start(to[0:U], fro.rearrange("(p n) -> p n", p=U)).then_inc(s_e, 16)
            for c in range(CHUNKS):
                sp.dma_start(x_all[0:U, CHUNK * c:CHUNK * c + CHUNK, :],
                             x.rearrange("(u p) d -> p u d", p=U)[:, CHUNK * c:CHUNK * c + CHUNK, :]
                             ).then_inc(s_x[c], 16)
            loads = [
                (wqkv_s[:], wqkv.rearrange("(k p) n -> p k n", p=P)),
                (wout_s[:], wout.rearrange("(k p) n -> p k n", p=P)),
                (gnnw_s[:], gnn_w.rearrange("(k p) n -> p k n", p=P)),
                (sw1_s[:], sw1.rearrange("(k p) n -> p k n", p=P)),
                (sw2_s[:], sw2.rearrange("(k p) n -> p k n", p=P)),
                (sw3_s[:], sw3),
                (ew1_s[:, 0], ew1[:, 0:P].rearrange("e p h -> p e h")),
                (ew1_s[:, 1], ew1[:, P:2 * P].rearrange("e p h -> p e h")),
                (ew2_s[:], ew2.rearrange("e p h -> p e h")),
                (ew3_s[:], ew3.rearrange("(q h) g o -> (h g) q o", h=2)),
                (gw_s[:], gw.rearrange("(k p) n -> p k n", p=P)),
                (sb1_s[:], sb1.rearrange("(k p) -> p k", p=P)),
                (sb2_s[:], sb2.rearrange("(p a) -> p a", a=1)),
                (eb1_s[:], eb1.rearrange("e p -> p e")),
                (eb2_s[:], eb2.rearrange("(q h) g -> (h g) q", h=2)),
                (b5_s[0:NE], eb3),
                (b5_s[NE:NE + 1], sb3.rearrange("(a d) -> a d", a=1)),
                (gamma_b[:], gamma.rearrange("(a d) -> a d", a=1).to_broadcast([P, D])),
                (gnnb_b[:], gnn_b.rearrange("(a d) -> a d", a=1).to_broadcast([P, D])),
                (alpha_b[:], alpha.rearrange("r a -> a r").to_broadcast([P, R])),
                (gb_b[:], gb.rearrange("(a d) -> a d", a=1).to_broadcast([P, NE])),
            ]
            assert len(loads) == NW + 1
            for to, fro in loads:
                sp.dma_start(to, fro).then_inc(s_w, 16)

            def rows_of(u):
                return u * U if isinstance(u, int) else sp.snap(u * U)

            t = Tally(sp, s_order["sp"])
            def p1(c, warm):
                at = c * CHUNK if not warm else sp.snap(c * CHUNK)
                at5 = c * CHUNK + GROUP if not warm else sp.snap(c * CHUNK + GROUP)
                for g, a in ((0, at), (1, at5)):
                    sp.wait_ge(n_trc, c * CHUNK + GROUP * (g + 1))
                    sp.dma_start(xnt_dram[:, bass.ds(a, GROUP), :],
                                 xnt_ring[:, GROUP * g:GROUP * g + GROUP].rearrange("p m k n -> p m (k n)")
                                 ).then_inc(n_tstore[g], 16)
                sp.wait_ge(n_xn, c * CHUNK + CHUNK)
                sp.dma_start(xn_dram.rearrange("(u p) d -> p u d", p=U)[:, bass.ds(at, CHUNK), :],
                             x_all[0:U, bass.ds(at, CHUNK), :]).then_inc(n_store, 16)
            repeat(sp, t, p1, 0, CHUNKS)

            def xb(b, warm):
                at = [rows_of(2 * b + s) for s in range(2)]
                for s in range(2):
                    if warm:
                        sp.wait_ge(b_sum, 2 * b + s - 1)
                    sp.dma_start(xin[0:U, s], x[bass.ds(at[s], U), :]).then_inc(b_ld[s], 16)
                for s in range(2):
                    sp.wait_ge(b_sum, 2 * b + s + 1)
                    sp.dma_start(xb_dram[bass.ds(at[s], U), :], t2[0:U, s]).then_inc(b_st[s], 16)
            repeat(sp, t, xb, 0, PAIRS)
            for s in range(2):
                sp.wait_ge(n_tstore[s], 16 * CHUNKS)
                sp.wait_ge(b_st[s], 16 * PAIRS)

            def load_xnt(b, freed, count, warm):
                at = 2 * b if not warm else sp.snap(2 * b)
                if count is not None:
                    sp.wait_ge(freed, count)
                sp.dma_start(xnt[:].rearrange("p s k n -> p s (k n)"),
                             xnt_dram[:, bass.ds(at, 2), :]).then_inc(s_tl, 16)

            def p2(b, warm):
                load_xnt(b, c_kv, 2 * b if warm else None, warm)
            repeat(sp, t, p2, 0, PAIRS)

            def p3(b, warm):
                at = [rows_of(2 * b + s) for s in range(2)]
                if warm:
                    load_xnt(b, q_q, 2 * b, warm)
                else:
                    load_xnt(b, c_kv, UNITS, warm)
                for s in range(2):
                    if warm:
                        sp.wait_ge(q_base, 2 * b)
                    sp.dma_start(xin[0:U, s], xb_dram[bass.ds(at[s], U), :]).then_inc(s_xl[s], 16)
                for s in range(2):
                    sp.wait_ge(q_base, 2 * b + s + 1)
                    sp.dma_start(base_dram[bass.ds(at[s], U), :], t2[0:U, s]).then_inc(s_stored[s], 16)
            repeat(sp, t, p3, 0, PAIRS)
            for s in range(2):
                sp.wait_ge(s_stored[s], 16 * PAIRS)

            sp.wait_ge(g_idx, 2)
            final = FinalUnits(nc, sp, first, RING, U, UNITS)

            def load_base(n):
                at = sp.snap(n * U)
                sp.wait_ge(q_base, n + UNITS)
                sp.dma_start(xin[0:U, 0], base_dram[bass.ds(at, U), :]).then_inc(s_xl[0], 16)
                final.begin()
            with sp.Fori(2 * PAIRS, BODIES) as i:
                with final.due(i):
                    n = final.next()
                    load_base(n)
            with sp.Fori(0, UNITS) as i:
                with final.left():
                    n = final.next()
                    load_base(n)
            sp.wait_ge(s_stored[0], 16 * PAIRS + 16 * UNITS)

        @block.gpsimd
        def _(pool):
            t = Tally(pool, s_pl)
            t.mark(pool.memset(ident[:], 0.0))
            t.mark(pool.memset(ones[:], 1.0))
            t.mark(pool.memset(half_pow[:], -0.5))
            pool.memset(zeros[:], 0.0).then_inc(s_const, 1)
            t.mark(pool.memset(g5[:], 1.0))
            t.mark(pool.memset(before[:], 1.0))
            t.settle()
            pool.affine_select(out=ident[:], in_=ident[:], compare_op=ALU.not_equal, fill=1.0, base=0,
                               pattern=[[-1, P]], channel_multiplier=1).then_inc(s_const, 1)
            pool.affine_select(out=before[:], in_=before[:], compare_op=ALU.is_gt, fill=0.0, base=0,
                               pattern=[[1, NE], [-1, NE]], channel_multiplier=0).then_inc(s_const, 1)
            pool.iota(iota_p[:], [[0, 1]], base=0, channel_multiplier=1).then_inc(s_const, 1)
            pool.iota(expert_i[:], [[2, 2], [1, 2], [0, EH2]], base=0, channel_multiplier=-1).then_inc(s_const, 1)
            pool.iota(nodes[:], [[1, WIDE]], base=0, channel_multiplier=0,
                      allow_small_or_imprecise_dtypes=True).then_inc(s_const, 1)
            pool.iota(node_s[0:U], [[1, NCOLS]], base=0, channel_multiplier=NCOLS).then_inc(s_const, 1)

            pool.wait_ge(n_var, 1)
            pool.tensor_tensor(rstd_all[0:U], var_all[0:U], half_pow[0:U].to_broadcast([U, UNITS]),
                               ALU.pow).then_inc(n_rstd, 1)

            pool.wait_ge(s_w, 16 * (NW + 1))

            def xb(b, warm):
                for s in range(2):
                    if warm:
                        pool.wait_ge(b_st[s], 16 * b)
                    pool.wait_ge(b_ld[s], 16 * b + 16)
                    pool.tensor_tensor(t2[0:U, s], xin[0:U, s], gnnb_b[0:U], ALU.add).then_inc(b_sum, 1)
            repeat(pool, t, xb, 0, PAIRS)

            pool.wait_ge(n_store, 16 * CHUNKS)
            pool.wait_ge(n_cp, UNITS)
            pool.memset(agg[:], 0.0).then_inc(n_zero, 1)
            for s in range(2):
                pool.wait_ge(n_tstore[s], 16 * CHUNKS)
            pool.wait_ge(n_kt, UNITS)

            def gathers(i, warm):
                for j in range(RING):
                    if j % HALF == 0:
                        t.settle()
                        pool.wait_ge(g_idx, 2 * i + j // HALF + 1)
                        t.mark(pool.tensor_tensor(carrier[0:1], half_pow[0:1], half_pow[0:1], ALU.add))
                    pool.indirect_dma_start(gath[:, j], None, xn_dram[:, :],
                                            bass.IndirectOffsetOnAxis(ap=cols[:, j:j + 1], axis=0)).then_inc(g_in[j], 16)
            repeat(pool, t, gathers, 0, BODIES)

        @block.scalar
        def _(act):
            act.wait_ge(s_const, 7)
            act.wait_ge(s_w, 16 * (NW + 1))

            t = Tally(act, s_order["act"])

            def p1(c, warm):
                for m in range(CHUNK + 1):
                    u = c * CHUNK + m
                    if m < CHUNK:
                        act.wait_ge(n_xn, u + 1)
                        if warm or m >= 2:
                            act.wait_ge(n_tr, u - 1)
                        act.copy(t0[0:U, m % 2], x_all[0:U, bass.ds(u, 1), :].rearrange("p a d -> p (a d)")
                                 ).then_inc(n_cp, 1)
                    if m >= 1:
                        act.wait_ge(n_tr, u)
                        if warm and m == 1:
                            act.wait_ge(n_tstore[0], 16 * c)
                            act.wait_ge(n_kt, c * CHUNK)
                        if warm and m == GROUP + 1:
                            act.wait_ge(n_tstore[1], 16 * c)
                        act.copy(xnt_ring[:, m - 1], bank[(m - 1) % 2][:, 0:K2 * U].rearrange("p (k n) -> p k n", k=K2)
                                 ).then_inc(n_trc, 1)
            repeat(act, t, p1, 0, CHUNKS)
            act.wait_ge(m_row, 1)
            act.copy(nkrow[:], bank[2][0:1, 0:D].rearrange("p (k n) -> p k n", k=K2)).then_inc(m_rowc, 1)

            for n, (to, signs) in enumerate(turns):
                for q in range(2):
                    act.wait_ge(s_turn, 4 * n + q + 1)
                    for lo, hi, sc in signs[q]:
                        last = act.activation((sort_a, sort_b)[to][:, lo:hi], bank[q][:, lo - 512 * q:hi - 512 * q],
                                              ACT.Copy, scale=sc)
                    last.then_inc(s_eva, 1)

            def p2(b, warm):
                for s in range(2):
                    u = 2 * b + s
                    act.wait_ge(c_kv, u + 1)
                    if warm:
                        act.wait_ge(c_ctx, u - 1)
                    act.activation(t0[0:U, s], bank[4 + s][0:U, 0:D], ACT.Exp).then_inc(c_exp, 1)
                    act.copy(t1[0:U, s], bank[4 + s][0:U, D:2 * D]).then_inc(c_v, 1)
            repeat(act, t, p2, 0, PAIRS)

            def p3(b, warm):
                for s in range(2):
                    u = 2 * b + s
                    act.wait_ge(q_sub, u + 1)
                    if warm:
                        act.wait_ge(q_tr, u - 1)
                    for h in range(HEADS):
                        last = act.activation(t0[0:U, s, h * DH:(h + 1) * DH], bank[4 + s][0:U, h * DH:(h + 1) * DH],
                                              ACT.Exp, bias=head[0:U, s, 2, h:h + 1])
                    last.then_inc(q_exp, 1)
                for s in range(2):
                    u = 2 * b + s
                    act.wait_ge(q_tr, u + 1)
                    if warm:
                        act.wait_ge(q_o, u - 1)
                    act.copy(h1t[:, s], bank[4 + s][:, 0:K2 * U].rearrange("p (k n) -> p k n", k=K2)).then_inc(q_trc, 1)
            repeat(act, t, p3, 0, PAIRS)

            final = FinalUnits(nc, act, first, RING, U, UNITS)

            def weights_out(n):
                act.wait_ge(f_gt, n)
                act.copy(g5t[:, 0], bank[5][0:NE + 1, GT0:GT0 + U]).then_inc(f_gtc, 1)

            def result_out(n):
                at = n * U - U if isinstance(n, int) else act.snap(nc.s_assert_within(n * U - U, 0, N - U))
                act.wait_ge(f_res, n + 1)
                act.dma_start(out[bass.ds(at, U), :], t2[0:U, 0]).then_inc(s_stored[0], 16)

            def unit(i, n):
                with act.If(n > 0):
                    weights_out(n)
                act.wait_ge(g_acc, i * RING)
                act.copy(xnt[:, 0], agg[:, :, bass.ds(n * U, U)]).then_inc(f_ag, 1)
                with act.If(n > 0):
                    result_out(n)
                act.wait_ge(f_tr, n + 1)
                act.copy(t3t[:, 0], bank[4][:, D:D + K2 * U].rearrange("p (k n) -> p k n", k=K2)).then_inc(f_znt, 1)
                act.wait_ge(f_h, n + 1)
                for k in range(K2):
                    act.activation(h1t[:, 0, k], bank[5][:, k * U:k * U + U], ACT.Relu, bias=sb1_s[:, k:k + 1])
                for e in range(NE):
                    last = act.activation(e1t[:, 0, e], bank[6][:, e * U:e * U + U], ACT.Relu, bias=eb1_s[:, e:e + 1])
                last.then_inc(f_relu, 1)
                act.wait_ge(f_gl, n + 1)
                act.activation(gs[0:U, 0, 1], gs[0:U, 0, 0], ACT.Exp).then_inc(f_ge, 1)
                act.wait_ge(f_p, n + 1)
                act.activation(gs[0:U, 0, 4], gs[0:U, 0, 3], ACT.Exp).then_inc(f_pe, 1)
                act.wait_ge(f_2, n + 1)
                act.activation(h2t[:, 0], bank[5][:, D:D + U], ACT.Relu, bias=sb2_s[:, 0:1]).then_inc(f_h2, 1)
                final.begin()
            for s in range(2):
                act.wait_ge(s_stored[s], 16 * PAIRS)
            with act.Fori(2 * PAIRS, BODIES) as i:
                with final.due(i):
                    n = final.next()
                    unit(i, n)
            with act.Fori(0, UNITS) as i:
                with final.left():
                    n = final.next()
                    unit(BODIES, n)
            weights_out(UNITS)
            result_out(UNITS)

        @block.vector
        def _(dve):
            t = Tally(dve, s_v)

            def do(ins):
                t.mark(ins)
                t.settle()

            V = nc.vector
            dve.wait_ge(s_const, 7)
            dve.wait_ge(s_w, 16 * (NW + 1))
            for b in range(7):
                t.mark(V.tensor_scalar(bit_i[:, b:b + 1], iota_p[:], b, 1, ALU.logical_shift_right, ALU.bitwise_and))
            t.mark(V.memset(kmax[:], -3.0e38))
            t.mark(V.tensor_scalar(spread[:].rearrange("e q p -> e (q p)"),
                                   expert_i[:].rearrange("e q h g -> e (q h g)"), 0.0, None, ALU.is_equal))
            t.settle()
            do(V.tensor_scalar(sign[:], bit_i[:], -2.0, 1.0, ALU.mult, ALU.add))
            V.memset(ctx_t[:], 0.0).then_inc(s_constv, 1)

            dve.wait_ge(s_e, 48)
            A, B = sort_a, sort_b
            Ai, Bi = A[:].bitcast(I32), B[:].bitcast(I32)
            pad = BIAS | PAD_ROW << ROW_SHIFT | R
            t.mark(V.memset(Ai, pad))
            do(V.tensor_scalar(typ_s[0:U], typ_s[0:U], BIAS, None, ALU.bitwise_or))
            for row, col, c0 in ((src_s, dst_s, 0), (dst_s, src_s, ECOLS)):
                do(V.tensor_scalar(mid_s[0:U], col[0:U], COL_SHIFT, None, ALU.logical_shift_left))
                do(V.tensor_tensor(mid_s[0:U], mid_s[0:U], typ_s[0:U], ALU.bitwise_or))
                do(V.tensor_scalar(Ai[0:U, c0:c0 + ECOLS], row[0:U], ROW_SHIFT, None, ALU.logical_shift_left))
                do(V.tensor_tensor(Ai[0:U, c0:c0 + ECOLS], Ai[0:U, c0:c0 + ECOLS], mid_s[0:U], ALU.bitwise_or))
            own = Ai[0:U, 2 * ECOLS:2 * ECOLS + NCOLS]
            do(V.tensor_scalar(own, node_s[0:U], ROW_SHIFT, BIAS | R, ALU.logical_shift_left, ALU.bitwise_or))
            do(V.tensor_scalar(node_s[0:U], node_s[0:U], COL_SHIFT, None, ALU.logical_shift_left))
            do(V.tensor_tensor(own, own, node_s[0:U], ALU.bitwise_or))
            do(V.tensor_scalar(A[:], A[:], sign[:, 0:1], None, ALU.mult))

            buf = [A, B]
            at = 0
            nready = 0

            def compare(j, k, negated=False, ready=False):
                nonlocal at, nready
                todo = []

                def pick(y, x0, x1, op):
                    todo.append((y, x0, x1, op))
                a, o = buf[at], buf[1 - at]
                i = 1 << j
                if k is None:
                    va, vo = (z[:].rearrange("p (o t i) -> p o t i", t=2, i=i) for z in (a, o))
                    pick(vo[:, :, 0], va[:, :, 0], va[:, :, 1], ALU.min)
                    pick(vo[:, :, 1], va[:, :, 0], va[:, :, 1], ALU.max)
                else:
                    m = 1 << (k - j - 1)
                    va, vo = (z[:].rearrange("p (o d m t i) -> p o d m t i", d=2, m=m, t=2, i=i) for z in (a, o))
                    for d in range(2):
                        for lo in range(2):
                            op = ALU.min if lo == d else ALU.max
                            mid = 0 if m == 1 else slice(0, m)
                            pick(vo[:, :, d, mid, lo], va[:, :, d, mid, 0], va[:, :, d, mid, 1], op)
                for n, (y, x0, x1, op) in enumerate(todo):
                    if negated:
                        ins = V.scalar_tensor_tensor(y, x1, -1.0, x0, ALU.mult, op)
                    else:
                        ins = V.tensor_tensor(y, x0, x1, op)
                    if ready and n == len(todo) - 1:
                        ins.then_inc(s_key, 1)
                        nready += 1
                        dve.wait_ge(s_key, nready)
                    else:
                        t.mark(ins)
                t.settle()
                at = 1 - at

            nturn = 0

            def turn():
                nonlocal at, nturn
                signs = turns[nturn][1]
                for q in range(2, 4):
                    dve.wait_ge(s_turn, 4 * nturn + q + 1)
                    for lo, hi, sc in signs[q]:
                        t.mark(V.tensor_scalar(buf[1 - at][:, lo:hi], bank[q][:, lo - 512 * q:hi - 512 * q], sc, None,
                                               ALU.mult))
                t.settle()
                nturn += 1
                dve.wait_ge(s_eva, 2 * nturn)
                at = 1 - at

            for k in range(1, 8):
                for j in range(k - 1, -1, -1):
                    compare(j, k if k < 7 else None, ready=(k == 7 and j == 0))
            for c in range(CHUNKS):
                dve.wait_ge(s_x[c], 16)
                with dve.Fori(CHUNK * c, CHUNK * c + CHUNK) as u:
                    V.bn_stats(stats_all[0:U, bass.ds(u, 1)].rearrange("p a d -> p (a d)"),
                               x_all[0:U, bass.ds(u, 1)].rearrange("p a d -> p (a d)")).then_inc(n_stat, 1)
            dve.wait_ge(n_stat, UNITS)
            st = stats_all[0:U]
            mean_e, m2_e, mean_o, m2_o = st[:, :, 1], st[:, :, 2], st[:, :, 4], st[:, :, 5]
            mean, var, dif = mean_all[0:U], var_all[0:U], dif_all[0:U]
            t.mark(V.tensor_tensor(mean, mean_e, mean_o, ALU.add))
            t.mark(V.tensor_tensor(dif, mean_e, mean_o, ALU.subtract))
            do(V.tensor_tensor(var, m2_e, m2_o, ALU.add))
            t.mark(V.tensor_scalar(mean, mean, 0.5, None, ALU.mult))
            do(V.scalar_tensor_tensor(dif, dif, 0.25, dif, ALU.mult, ALU.mult))
            do(V.scalar_tensor_tensor(var, var, 1.0 / D, dif, ALU.mult, ALU.add))
            V.tensor_scalar(var, var, EPS, None, ALU.add).then_inc(n_var, 1)
            dve.wait_ge(n_rstd, 1)
            KLAG = 4

            def p1(c, warm):
                for m in range(CHUNK + KLAG):
                    u = c * CHUNK + m
                    if m < CHUNK:
                        xu = x_all[0:U, bass.ds(u, 1)].rearrange("p a d -> p (a d)")
                        V.tensor_scalar(xu, xu, mean_all[0:U, bass.ds(u, 1)], rstd_all[0:U, bass.ds(u, 1)],
                                        ALU.subtract, ALU.mult).then_inc(n_xn, 1)
                    if m >= KLAG:
                        dve.wait_ge(n_kt, u - KLAG + 1)
                        dve.wait_ge(n_kmax, u - KLAG)
                        V.tensor_tensor(kmax[:], bank[3 + (m - KLAG) % 5][:, 0:K2 * U].rearrange("p (k n) -> p k n", k=K2),
                                        kmax[:], ALU.max).then_inc(n_kmax, 1)
            repeat(dve, t, p1, 0, CHUNKS)
            dve.wait_ge(n_kmax, UNITS)
            do(V.tensor_reduce(nkmax[:], kmax[:], AX.X, ALU.max))
            V.tensor_scalar(nkmax[:], nkmax[:], -1.0, None, ALU.mult).then_inc(m_neg, 1)

            for k in range(8, BITS + 1):
                turn()
                for j in range(k - 1, 6, -1):
                    compare(j - 7, None if k == BITS else k - 7, negated=(j == k - 1), ready=(j == 7))
                turn()
                for j in range(6, -1, -1):
                    compare(j, None, ready=(j == 0))
            turn()
            assert nturn == len(turns)
            S, T = buf[at], buf[1 - at]
            Si, Ti = S[:].bitcast(I32), T[:].bitcast(I32)

            do(V.tensor_scalar(Ti, Si, ROW_SHIFT, ID_MASK, ALU.logical_shift_right, ALU.bitwise_and))
            t.mark(V.tensor_copy(row_f[:], Ti))
            do(V.tensor_scalar(first[:], Ti[0:1], float(N - 1), None, ALU.min))
            do(V.tensor_scalar(Ti, Si, REL_MASK, None, ALU.bitwise_and))
            dve.wait_ge(n_zero, 1)
            for s in range(2):
                dve.wait_ge(n_tstore[s], 16 * CHUNKS)
            tmp = gath_flat[:, 0:COLS]
            for r in range(R):
                if r == 0:
                    do(V.tensor_scalar(wgt[:], Ti, 0.0, alpha_b[:, 0:1], ALU.is_equal, ALU.mult))
                else:
                    do(V.tensor_scalar(tmp, Ti, float(r), alpha_b[:, r:r + 1], ALU.is_equal, ALU.mult))
                    do(V.tensor_tensor(wgt[:], wgt[:], tmp, ALU.add))
            def unpack_cols(tile0, j0):
                V.tensor_scalar(cols[:, j0:j0 + HALF], Si[:, bass.ds(tile0, HALF)], COL_SHIFT, ID_MASK,
                                ALU.logical_shift_right, ALU.bitwise_and).then_inc(g_idx, 1)
            unpack_cols(0, 0)
            unpack_cols(HALF, HALF)

            def accumulate(tile, j, r0):
                dve.wait_ge(g_mm, tile + 1)
                dve.wait_ge(g_acc, tile)
                window = agg[:, :, bass.ds(r0, P)]
                V.tensor_tensor(window, bank[j % SUMS][:, 0:K2 * P].rearrange("p (k n) -> p k n", k=K2), window,
                                ALU.add).then_inc(g_acc, 1)

            def firsts(tile, count):
                _, vals = nc.values_load_multi_w_load_instructions(
                    first[0:1, bass.ds(tile, count)], engines=[dve.engine], min_val=0, max_val=N - 1,
                    skip_runtime_bounds_check_because="clamped to the last node when unpacked, and rows are not negative")
                return vals

            def gather_body(i, started, beside):
                before_rows = firsts(RING * i - LAG, LAG) if started else None
                for q in range(RING // LAG):
                    rows = firsts(RING * i + q * LAG, LAG)
                    for m in range(LAG):
                        j = q * LAG + m
                        tile = RING * i + j
                        V.tensor_scalar(hot[:, j], nodes[:, bass.ds(rows[m], P)], row_f[:, bass.ds(tile, 1)],
                                        wgt[:, bass.ds(tile, 1)], ALU.is_equal, ALU.mult).then_inc(g_hot, 1)
                        if before_rows:
                            accumulate(tile - LAG, (j - LAG) % RING, before_rows[m])
                        if j in beside:
                            beside[j]()
                    if q == 0 and started:
                        unpack_cols(RING * i + HALF, HALF)
                    if q == 2:
                        unpack_cols(RING * i + RING, 0)
                    before_rows = rows

            repeat(dve, t, lambda i, warm: gather_body(i, warm, {}), 0, PAIRS)

            dve.wait_ge(c_end, K2)
            for h in range(HEADS):
                k, p0 = h // 4, DH * (h % 4)
                t.mark(V.tensor_copy(ctx_t[p0:p0 + DH, k, p0:p0 + DH], bank[6 + k][p0:p0 + DH, h * DH:(h + 1) * DH]))
            for k in range(K2):
                t.mark(V.reciprocal(ksum_r[:, k:k + 1], bank[6 + k][:, D:D + 1]))
            t.settle()
            V.tensor_scalar(ksum_r[:], ksum_r[:], SCALE, None, ALU.mult).then_inc(w_ctx, 1)
            dve.wait_ge(w_ctx, 1)
            dve.wait_ge(w_mm, 1)
            for k in range(K2):
                V.tensor_scalar(mix_w[:, k], bank[4][:, k * D:k * D + D], ksum_r[:, k:k + 1], None,
                                ALU.mult).then_inc(w_done, 1)

            def moments(t, units):
                def do(ins):
                    t.mark(ins)
                    t.settle()
                for q, unit in enumerate(units):
                    t.mark(V.bn_stats(stats[0:U, q], unit))
                t.settle()
                w = len(units)
                st = stats[0:U, 0:w]
                mean, var, dif = mv[0:U, 0:w, 0], mv[0:U, 0:w, 1], mdif[0:U, 0:w]
                t.mark(V.tensor_tensor(mean, st[:, :, 1], st[:, :, 4], ALU.add))
                t.mark(V.tensor_tensor(dif, st[:, :, 1], st[:, :, 4], ALU.subtract))
                do(V.tensor_tensor(var, st[:, :, 2], st[:, :, 5], ALU.add))
                t.mark(V.tensor_scalar(mean, mean, 0.5, None, ALU.mult))
                do(V.scalar_tensor_tensor(dif, dif, 0.25, dif, ALU.mult, ALU.mult))
                do(V.scalar_tensor_tensor(var, var, 1.0 / D, dif, ALU.mult, ALU.add))
                do(V.tensor_scalar(var, var, EPS, None, ALU.add))
                y, a = rstd[0:U, 0:w, 0], newton[0:U, 0:w]
                do(V.tensor_scalar(y.bitcast(I32), var.bitcast(I32), 1, None, ALU.logical_shift_right))
                do(V.tensor_scalar(y.bitcast(I32), y.bitcast(I32), -1.0, float(0x5F3759DF), ALU.mult, ALU.add))
                for _ in range(3):
                    do(V.tensor_tensor(a, y, y, ALU.mult))
                    do(V.scalar_tensor_tensor(a, a, -0.5, var, ALU.mult, ALU.mult))
                    do(V.scalar_tensor_tensor(y, a, 1.5, y, ALU.add, ALU.mult))

            def mix_norm(b):
                for s in range(2):
                    dve.wait_ge(q_o, 2 * b + s + 1)
                moments(t, [bank[6][0:U, 0:D], bank[7][0:U, 0:D]])
                for s in range(2):
                    V.scalar_tensor_tensor(t1[0:U, s], bank[6 + s][0:U, 0:D], mv[0:U, s, 0:1], gamma_b[0:U],
                                           ALU.subtract, ALU.mult).then_inc(q_ln, 1)
                dve.wait_ge(q_ln, 2 * b + 2)
                for s in range(2):
                    dve.wait_ge(s_xl[s], 16 * b + 16)
                    dve.wait_ge(s_stored[s], 16 * b)
                    V.scalar_tensor_tensor(t2[0:U, s], t1[0:U, s], rstd[0:U, s], xin[0:U, s], ALU.mult,
                                           ALU.add).then_inc(q_base, 1)

            def p3_steps(b, warm):
                def heads_max():
                    for s in range(2):
                        q = bank[4 + s][0:U, 0:D].rearrange("p (h d) -> p h d", h=HEADS)
                        dve.wait_ge(q_q, 2 * b + s + 1)
                        t.mark(V.tensor_reduce(head[0:U, s, 0], q, AX.X, ALU.max))
                    t.settle()
                    for s in range(2):
                        V.tensor_scalar(head[0:U, s, 2], head[0:U, s, 0], -1.0, None, ALU.mult).then_inc(q_sub, 1)

                def heads_scale():
                    for s in range(2):
                        e = t0[0:U, s].rearrange("p (h d) -> p h d", h=HEADS)
                        dve.wait_ge(q_exp, 2 * b + s + 1)
                        do(V.tensor_reduce(head[0:U, s, 0], e, AX.X, ALU.add))
                        do(V.reciprocal(head[0:U, s, 1], head[0:U, s, 0]))
                        V.tensor_tensor(e, e, head[0:U, s, 1].unsqueeze(2).to_broadcast([U, HEADS, DH]),
                                        ALU.mult).then_inc(q_norm, 1)
                steps = {6: heads_max, 11: heads_scale}
                if warm:
                    steps[3] = lambda: mix_norm(b - 1)
                return steps

            gather_body(PAIRS, True, p3_steps(0, False))
            repeat(dve, t, lambda i, warm: gather_body(i, True, p3_steps(i - PAIRS, True)), PAIRS + 1, 2 * PAIRS)
            mix_norm(PAIRS - 1)
            final = FinalUnits(nc, dve, first, RING, U, UNITS)
            f = Tally(dve, f_order)
            V.memset(carrier[64:65], 0.0).then_inc(f_res, 1)
            HEAD_STEPS = 31

            def experts(n):
                dve.wait_ge(f_2, n)
                for q in range(NE // 2):
                    last = V.tensor_scalar(e2t[:, 0, q], bank[7][:, q * U:q * U + U], eb2_s[:, q:q + 1], 0.0,
                                           ALU.add, ALU.max)
                last.then_inc(f_e2, 1)
                dve.wait_ge(f_e2, n)
                dve.wait_ge(f_gb, n)
                V.tensor_tensor(e2g[:, 0], e2t[:, 0], bank[6][:, 0:2 * U].rearrange("p (q n) -> p q n", q=2),
                                ALU.mult).then_inc(f_e2g, 1)

            def result(n):
                dve.wait_ge(f_o, n)
                dve.wait_ge(s_stored[0], n * 16 + (16 * PAIRS - 16))
                V.tensor_tensor(t2[0:U, 0], bank[7][0:U, 0:D], t1[0:U, 0], ALU.add).then_inc(f_res, 1)

            def residual(n):
                assert f.marks % HEAD_STEPS == 0
                f.count = n * HEAD_STEPS
                dve.wait_ge(f_res, n + 1)
                dve.wait_ge(f_y, n + 1)
                dve.wait_ge(s_xl[0], n * 16 + (16 * PAIRS + 16))
                V.tensor_tensor(t1[0:U, 0], bank[4][0:U, 0:D], xin[0:U, 0], ALU.add).then_inc(q_base, 1)
                dve.wait_ge(q_base, n + (UNITS + 1))
                moments(f, [t1[0:U, 0]])
                V.tensor_scalar(t0[0:U, 0], t1[0:U, 0], mv[0:U, 0, 0:1], rstd[0:U, 0], ALU.subtract,
                                ALU.mult).then_inc(f_zn, 1)

            def gates(n):
                def do(ins):
                    f.mark(ins)
                    f.settle()
                g = gs[0:U, 0]
                h = head[0:U, 0, 0]
                dve.wait_ge(f_log, n + 1)
                do(V.tensor_tensor(g[:, 0], bank[4][0:U, 0:NE], gb_b[0:U], ALU.add))
                do(V.tensor_reduce(h[:, 0:1], g[:, 0], AX.X, ALU.max))
                V.tensor_scalar(g[:, 0], g[:, 0], h[:, 0:1], None, ALU.subtract).then_inc(f_gl, 1)
                dve.wait_ge(f_ge, n + 1)
                do(V.tensor_reduce(h[:, 0:1], g[:, 1], AX.X, ALU.add))
                do(V.reciprocal(h[:, 1:2], h[:, 0:1]))
                V.tensor_scalar(g[:, 3], g[:, 1], h[:, 1:2], None, ALU.mult).then_inc(f_p, 1)
                dve.wait_ge(f_p, n + 1)
                mine = g[:, 3].unsqueeze(2).to_broadcast([U, NE, NE])
                other = g[:, 3].unsqueeze(1).to_broadcast([U, NE, NE])
                sq = gsq[0:U, 0]
                f.mark(V.tensor_tensor(sq[:, 0], other, mine, ALU.is_gt))
                do(V.tensor_tensor(sq[:, 1], other, mine, ALU.is_equal))
                do(V.tensor_tensor(sq[:, 1], sq[:, 1], before[0:U], ALU.mult))
                do(V.tensor_tensor(sq[:, 2], sq[:, 1], sq[:, 0], ALU.add))
                do(V.tensor_reduce(g[:, 5], sq[:, 2], AX.X, ALU.add))
                dve.wait_ge(f_pe, n + 1)
                do(V.scalar_tensor_tensor(g[:, 6], g[:, 5], 1.5, g[:, 4], ALU.is_lt, ALU.mult))
                do(V.tensor_reduce(h[:, 2:3], g[:, 6], AX.X, ALU.add))
                do(V.reciprocal(h[:, 3:4], h[:, 2:3]))
                V.tensor_scalar(g5[0:U, 0, 0:NE], g[:, 6], h[:, 3:4], None, ALU.mult).then_inc(f_g, 1)

            def after_first(n, step):
                def run():
                    with dve.If(n > 0):
                        step(n)
                return run

            def unit_steps(n):
                def both():
                    after_first(n, result)()
                    residual(n)
                return {3: after_first(n, experts), 9: both, 14: lambda: gates(n)}

            with dve.Fori(2 * PAIRS, BODIES) as i:
                with final.due(i):
                    n = final.next()
                    gather_body(i, True, unit_steps(n))
                    final.begin()
                with dve.Else():
                    gather_body(i, True, {})
            rows = firsts(RING * BODIES - LAG, LAG)
            for m in range(LAG):
                accumulate(RING * BODIES - LAG + m, RING - LAG + m, rows[m])
            with dve.Fori(0, UNITS) as i:
                with final.left():
                    n = final.next()
                    steps = unit_steps(n)
                    for j in sorted(steps):
                        steps[j]()
                    final.begin()
            experts(UNITS)
            result(UNITS)

        @block.tensor
        def _(pe):
            M = nc.tensor.matmul
            pe.wait_ge(s_const, 7)
            pe.wait_ge(s_w, 16 * (NW + 1))

            def turn_unit(src_ap, s, to, o, done):
                for k in range(K2):
                    last = pe.transpose(to[:, o + k * U:o + k * U + U], src_ap[:, k * P:(k + 1) * P], ident[0:U, 0:U])
                last.then_inc(done, 1)

            t = Tally(pe, s_order["pe"])

            def p1(c, warm):
                for m in range(CHUNK + 1):
                    u = c * CHUNK + m
                    if m < CHUNK:
                        pe.wait_ge(n_cp, u + 1)
                        if warm or m >= 2:
                            pe.wait_ge(n_trc, u - 1)
                        turn_unit(t0[0:U, m % 2], 0, bank[m % 2], 0, n_tr)
                    if m >= 1:
                        pe.wait_ge(n_trc, u)
                        if warm or m >= 6:
                            pe.wait_ge(n_kmax, u - 5)
                        for f in range(K2):
                            for k in range(K2):
                                last = M(bank[3 + (m - 1) % 5][:, f * U:f * U + U],
                                         wqkv_s[:, k, D + f * P:D + f * P + P], xnt_ring[:, m - 1, k],
                                         start=(k == 0), stop=(k == K2 - 1))
                        last.then_inc(n_kt, 1)
            repeat(pe, t, p1, 0, CHUNKS)
            pe.wait_ge(m_neg, 1)
            for k in range(K2):
                last = pe.transpose(bank[2][0:1, k * P:(k + 1) * P], nkmax[:, k:k + 1], ident[:])
            last.then_inc(m_row, 1)
            pe.wait_ge(m_rowc, 1)

            for n, (to, _) in enumerate(turns):
                pe.wait_ge(s_key, n + 1)
                for q in range(4):
                    for c in range(4 * q, 4 * q + 4):
                        last = pe.transpose(bank[q][:, (c - 4 * q) * P:(c - 4 * q + 1) * P],
                                            (sort_a, sort_b)[1 - to][:, c * P:(c + 1) * P], ident[:])
                    last.then_inc(s_turn, 1)

            def sums(i, started, beside):
                for j in range(RING):
                    tile = RING * i + j
                    if j in beside:
                        beside[j]()
                    pe.wait_ge(g_in[j], 16 * i + 16)
                    pe.wait_ge(g_hot, tile + 1)
                    if started or j >= SUMS:
                        pe.wait_ge(g_acc, tile - SUMS + 1)
                    elif j == 0:
                        pe.wait_ge(s_eva, 2 * len(turns))
                    for k in range(K2):
                        last = M(bank[j % SUMS][:, k * P:(k + 1) * P], gath[:, j, k * P:(k + 1) * P], hot[:, j],
                                 start=True, stop=True)
                    last.then_inc(g_mm, 1)

            def p2_steps(b, warm):
                def kv():
                    pe.wait_ge(s_tl, 16 * b + 16)
                    for s in range(2):
                        u = 2 * b + s
                        if warm:
                            pe.wait_ge(c_v, u - 1)
                        for k in range(K2):
                            M(bank[4 + s][0:U, D:2 * D], xnt[:, s, k], wqkv_s[:, k, 2 * D:3 * D], start=(k == 0),
                              stop=(k == K2 - 1))
                        for k in range(K2):
                            M(bank[4 + s][0:U, 0:D], xnt[:, s, k], wqkv_s[:, k, D:2 * D], start=(k == 0), stop=False)
                        M(bank[4 + s][0:U, 0:D], ones[0:1, 0:U], nkrow[:].rearrange("p k n -> p (k n)"), start=False,
                          stop=True).then_inc(c_kv, 1)

                def context():
                    for s in range(2):
                        u = 2 * b + s
                        pe.wait_ge(c_exp, u + 1)
                        pe.wait_ge(c_v, u + 1)
                        for k in range(K2):
                            M(bank[6 + k][:, 0:D], t1[0:U, s, k * P:(k + 1) * P], t0[0:U, s],
                              start=not warm and s == 0, stop=False, skip_group_check=True)
                            last = M(bank[6 + k][:, D:D + 1], t0[0:U, s, k * P:(k + 1) * P], ones[0:U, 0:1],
                                     start=False, stop=False, skip_group_check=True)
                        last.then_inc(c_ctx, 1)
                return {1: kv, 9: context}
            repeat(pe, t, lambda i, warm: sums(i, warm, p2_steps(i, warm)), 0, PAIRS)
            for k in range(K2):
                M(bank[6 + k][:, 0:D], zeros[:], b5_s[0:1], start=False, stop=True, skip_group_check=True)
                M(bank[6 + k][:, D:D + 1], zeros[:], ones[0:1, 0:1], start=False, stop=True,
                  skip_group_check=True).then_inc(c_end, 1)
            pe.wait_ge(w_ctx, 1)
            pe.wait_ge(s_constv, 1)
            for k in range(K2):
                last = M(bank[4][:, k * D:k * D + D], ctx_t[:, k], wout_s[:, k], start=True, stop=True)
            last.then_inc(w_mm, 1)
            pe.wait_ge(w_done, K2)

            def p3_steps(b, warm):
                def query():
                    pe.wait_ge(s_tl, 16 * (PAIRS + 1) + 16 * b)
                    for s in range(2):
                        if warm:
                            pe.wait_ge(q_trc, 2 * b + s - 1)
                        for k in range(K2):
                            last = M(bank[4 + s][0:U, 0:D], xnt[:, s, k], wqkv_s[:, k, 0:D], start=(k == 0),
                                     stop=(k == K2 - 1))
                        last.then_inc(q_q, 1)

                def turn_query():
                    for s in range(2):
                        pe.wait_ge(q_norm, 2 * b + s + 1)
                        turn_unit(t0[0:U, s], s, bank[4 + s], 0, q_tr)

                def mix():
                    for s in range(2):
                        pe.wait_ge(q_trc, 2 * b + s + 1)
                        if warm:
                            pe.wait_ge(q_ln, 2 * b)
                        for k in range(K2):
                            last = M(bank[6 + s][0:U, 0:D], h1t[:, s, k], mix_w[:, k], start=(k == 0),
                                     stop=(k == K2 - 1))
                        last.then_inc(q_o, 1)
                return {1: query, 12: turn_query, 15: mix}
            repeat(pe, t, lambda i, warm: sums(i, True, p3_steps(i - PAIRS, warm)), PAIRS, 2 * PAIRS)
            final = FinalUnits(nc, pe, first, RING, U, UNITS)

            def turn_weights(n):
                pe.wait_ge(f_g, n)
                pe.wait_ge(f_h2, n)
                pe.transpose(bank[5][0:NE + 1, GT0:GT0 + U], g5[0:U, 0], ident[0:U, 0:U]).then_inc(f_gt, 1)

            def spread_weights(n):
                pe.wait_ge(f_gtc, n)
                for q in range(NE // 2):
                    last = M(bank[6][:, q * U:q * U + U], spread[:, q], g5t[0:NE, 0], start=True, stop=True)
                last.then_inc(f_gb, 1)

            def mlp_out(n):
                pe.wait_ge(f_e2g, n)
                M(bank[7][0:U, 0:D], h2t[:, 0], sw3_s[:], start=True, stop=False)
                M(bank[7][0:U, 0:D], g5t[:, 0], b5_s[:], start=False, stop=False)
                for q in range(NE // 2):
                    last = M(bank[7][0:U, 0:D], e2g[:, 0, q], ew3_s[:, q], start=False, stop=(q == 1))
                last.then_inc(f_o, 1)

            def graph_out(n):
                pe.wait_ge(f_ag, n + 1)
                for k in range(K2):
                    last = M(bank[4][0:U, 0:D], xnt[:, 0, k], gnnw_s[:, k], start=(k == 0), stop=(k == K2 - 1))
                last.then_inc(f_y, 1)

            def turn_z(n):
                pe.wait_ge(f_zn, n + 1)
                turn_unit(t0[0:U, 0], 0, bank[4], D, f_tr)

            def first_layers(n):
                pe.wait_ge(f_znt, n + 1)
                for k in range(K2):
                    last = M(bank[4][0:U, 0:NE], t3t[:, 0, k], gw_s[:, k], start=(k == 0), stop=(k == K2 - 1))
                last.then_inc(f_log, 1)
                for p in range(K2):
                    for k in range(K2):
                        M(bank[5][:, p * U:p * U + U], sw1_s[:, k, p * P:p * P + P], t3t[:, 0, k],
                          start=(k == 0), stop=(k == K2 - 1))
                for e in range(NE):
                    for k in range(K2):
                        last = M(bank[6][:, e * U:e * U + U], ew1_s[:, k, e], t3t[:, 0, k], start=(k == 0),
                                 stop=(k == K2 - 1))
                last.then_inc(f_h, 1)

            def second_layers(n):
                pe.wait_ge(f_relu, n + 1)
                for k in range(K2):
                    M(bank[5][:, D:D + U], sw2_s[:, k], h1t[:, 0, k], start=(k == 0), stop=(k == K2 - 1))
                for e in range(NE):
                    p0 = EH2 * (e % 2)
                    last = M(bank[7][p0:p0 + EH2, (e // 2) * U:(e // 2) * U + U], ew2_s[:, e], e1t[:, 0, e],
                             start=True, stop=True)
                last.then_inc(f_2, 1)

            def after_first(n, step):
                def run():
                    with pe.If(n > 0):
                        step(n)
                return run

            def unit_steps(n):
                def both():
                    after_first(n, mlp_out)()
                    graph_out(n)
                return {0: after_first(n, turn_weights), 1: after_first(n, spread_weights), 5: both,
                        11: lambda: turn_z(n), 12: lambda: first_layers(n), 15: lambda: second_layers(n)}

            with pe.Fori(2 * PAIRS, BODIES) as i:
                with final.due(i):
                    n = final.next()
                    sums(i, True, unit_steps(n))
                    final.begin()
                with pe.Else():
                    sums(i, True, {})
            with pe.Fori(0, UNITS) as i:
                with final.left():
                    n = final.next()
                    steps = unit_steps(n)
                    for j in sorted(steps):
                        steps[j]()
                    final.begin()
            turn_weights(UNITS)
            spread_weights(UNITS)
            mlp_out(UNITS)


_INS = ["x", "src", "dst", "edge_type_11", "L0_gnn_weight", "L0_gnn_bias", "L0_gnn_alpha", "L0_mix_Wqkv",
        "L0_mix_Wout", "L0_mix_gamma", "L0_ffn_sW1", "L0_ffn_sb1", "L0_ffn_sW2", "L0_ffn_sb2", "L0_ffn_sW3",
        "L0_ffn_sb3", "L0_ffn_eW1", "L0_ffn_eb1", "L0_ffn_eW2", "L0_ffn_eb2", "L0_ffn_eW3", "L0_ffn_eb3",
        "L0_ffn_gW", "L0_ffn_gb"]


def kernel(**inputs):
    import numpy as _np
    import concourse.bacc as _bacc
    from concourse import mybir as _mybir
    from concourse.bass_utils import run_bass_kernel_spmd as _run

    nc = _bacc.Bacc("TRN2", target_bir_lowering=False, num_devices=1)
    arrays, args = {}, []
    for name in _INS:
        a = _np.ascontiguousarray(inputs[name])
        arrays[f"in_{name}_dram"] = a
        args.append(nc.dram_tensor(f"in_{name}_dram", a.shape, _mybir.dt.from_np(a.dtype), kind="ExternalInput").ap())
    shape = inputs["x"].shape
    args.append(nc.dram_tensor("out_0_dram", shape, _mybir.dt.float32, kind="ExternalOutput").ap())
    program(nc, *args)
    r = _run(nc, [arrays], core_ids=[0])
    return r.results[0]["out_0_dram"]
```

```python
from contextlib import ExitStack

import concourse.bass as bass
from concourse import mybir

F32 = mybir.dt.float32
I32 = mybir.dt.int32
ALU = mybir.AluOpType
ACT = mybir.ActivationFunctionType
AX = mybir.AxisListType

P = 128
EPS = 1e-5
HEADS = 8
COL_SHIFT, ROW_SHIFT, ID_BITS, REL_MASK = 4, 17, 13, 15
ID_MASK = (1 << ID_BITS) - 1
BIAS = 1 << 30
PAD_ROW = 8000


class Tally:

    def __init__(self, eng, sem):
        self.eng, self.sem, self.count, self.marks = eng, sem, 0, 0

    def mark(self, ins):
        ins.then_inc(self.sem, 1)
        self.count = self.count + 1
        self.marks += 1

    def settle(self):
        self.eng.wait_ge(self.sem, self.count)


class FinalUnits:

    def __init__(self, eng, unit_rows, units):
        self.eng = eng
        self.unit_rows, self.units = unit_rows, units
        self.begun = eng.alloc_register(f"units_begun_{eng.engine.name}")
        eng.reg_mov(self.begun, 0)

    def next(self):
        return self.eng.snap(self.begun, min_val=0, max_val=self.units - 1)

    def left(self):
        return self.eng.If(self.eng.snap(self.begun, min_val=0, max_val=self.units) < self.units)

    def run_left(self, unit):
        steps = 5
        with self.eng.Fori(0, self.units // steps):
            with self.left():
                with self.eng.Fori(0, steps):
                    with self.left():
                        unit(self.next())

    def begin(self):
        self.eng.reg_add(self.begun, self.begun, 1)

    def due(self, info):
        n = self.eng.snap(self.begun, min_val=0, max_val=self.units)
        return self.eng.If(n * self.unit_rows + (self.unit_rows - 1) < info[0])


def load_info(nc, eng, body_info, i, rows, count):
    _, vals = nc.values_load_multi_w_load_instructions(
        body_info[:].rearrange("o b c -> o (b c)")[0:1, bass.ds(i * 4, count)], engines=[eng.engine], min_val=0,
        max_val=rows - 1,
        skip_runtime_bounds_check_because="clamped to the last node when unpacked, and rows are not negative")
    return vals


def either(eng, tallies, case, one, other):
    at = [(t.count, t.marks) for t in tallies]
    with eng.If(case):
        one()
    ends = [t.marks for t in tallies]
    for t, (count, marks) in zip(tallies, at):
        t.count, t.marks = count, marks
    with eng.Else():
        other()
    assert ends == [t.marks for t in tallies]


def repeat(eng, tally, body, first, end):
    start = tally.count
    body(first, False)
    per = tally.count - start
    with eng.Fori(first + 1, end) as i:
        if per:
            tally.count = i * per + (start - first * per)
        body(i, True)
    tally.count = start + per * (end - first)


def program(nc, x, src, dst, edge_type, gnn_w, gnn_b, alpha, wqkv, wout, gamma,
            sw1, sb1, sw2, sb2, sw3, sb3, ew1, eb1, ew2, eb2, ew3, eb3, gw, gb, out):
    N, D = x.shape
    E = src.shape[0]
    R = alpha.shape[0]
    K2 = D // P
    U = 125
    UNITS = N // U
    PAIRS = UNITS // 2
    DH = D // HEADS
    SCALE = float(DH) ** -0.5
    NE, EH1, EH2 = ew1.shape[0], ew1.shape[2], ew2.shape[2]
    assert N % (2 * U) == 0 and D == 256 and E % U == 0 and N < PAD_ROW < 1 << ID_BITS
    ECOLS = E // U
    NCOLS = N // U
    MSGS = 2 * E + N
    BITS = (MSGS - 1).bit_length()
    COLS = (1 << BITS) // P
    BLOCKS = COLS // P
    TILES = -(-MSGS // P)
    RING = 16
    HALF = RING // 2
    WINDOW = 64
    HOT_AHEAD = 2
    BODIES = -(-TILES // RING)
    HALF_ACC = RING + 1
    BODY_ACC = 2 * HALF_ACC
    TILE_END = BODIES * RING + 1
    WCOLS = -(-BODIES * RING // (PAIRS + 1))
    assert RING <= WCOLS and WCOLS * (PAIRS + 1) <= COLS
    WIDE = -(-(N + P) // D) * D
    CHUNK = 10
    CHUNKS = UNITS // CHUNK
    GROUP = CHUNK // 2
    assert UNITS % CHUNK == 0 and UNITS * D <= K2 * WIDE and 4 * PAIRS < BODIES

    with ExitStack() as ctx:
        def sb(name, shape, dt=F32):
            return ctx.enter_context(nc.sbuf_tensor(name, shape, dt))

        def sem(name):
            return ctx.enter_context(nc.semaphore(name))

        ctx.enter_context(nc.allow_non_contiguous_dma(reason="bias columns of a few hundred elements"))

        xn_dram = nc.dram_tensor("xn_dram", (N, D), F32).ap()
        xnt_dram = nc.dram_tensor("xnt_dram", (P, UNITS, K2 * U), F32).ap()
        xb_dram = nc.dram_tensor("xb_dram", (N, D), F32).ap()
        base_dram = nc.dram_tensor("base_dram", (N, D), F32).ap()

        bank = [ctx.enter_context(nc.psum_tensor(f"bank{i}", [P, 512], F32)) for i in range(8)]

        wqkv_s = sb("wqkv_s", [P, K2, 3 * D])
        wout_s = sb("wout_s", [P, K2, D])
        gnnw_s = sb("gnnw_s", [P, K2, D])
        sw1_s = sb("sw1_s", [P, K2, D])
        sw2_s = sb("sw2_s", [P, K2, P])
        sw3_s = sb("sw3_s", [P, D])
        ew1_s = sb("ew1_s", [P, K2, NE, EH1])
        ew2_s = sb("ew2_s", [P, NE, EH2])
        ew3_s = sb("ew3_s", [P, NE // 2, D])
        gw_s = sb("gw_s", [P, K2, NE])
        sb1_s = sb("sb1_s", [P, K2])
        sb2_s = sb("sb2_s", [P, 1])
        eb1_s = sb("eb1_s", [P, NE])
        eb2_s = sb("eb2_s", [P, NE // 2])
        b5_s = sb("b5_s", [NE + 1, D])
        gamma_b = sb("gamma_b", [P, D])
        gnnb_b = sb("gnnb_b", [P, D])
        gb_b = sb("gb_b", [P, NE])
        alpha_b = sb("alpha_b", [P, R])
        ident = sb("ident", [P, P])
        ones = sb("ones", [P, P])
        zeros = sb("zeros", [1, P])
        iota_p = sb("iota_p", [P, 1], I32)
        bit_i = sb("bit_i", [P, 7], I32)
        sign = sb("sign", [P, 7])
        before = sb("before", [P, NE, NE])
        expert_i = sb("expert_i", [NE, 2, 2, EH2], I32)
        spread = sb("spread", [NE, NE // 2, P])
        carrier = sb("carrier", [P, 1])
        newton = sb("newton", [P, 2])
        mdif = sb("mdif", [P, 2])
        half_pow = sb("half_pow", [P, 1])
        nodes = sb("nodes", [P, WIDE])

        xin = sb("xin", [P, 2, D])
        xnt = sb("xnt", [P, 2, K2, U])
        t0 = sb("t0", [P, 2, D])
        t1 = sb("t1", [P, 2, D])
        t2 = sb("t2", [P, 2, D])
        stats = sb("stats", [P, 2, 6])
        mv = sb("mv", [P, 2, 2])
        rstd = sb("rstd", [P, 2, 1])
        n_stat = sem("n_stats")
        head = sb("head", [P, 2, 3, HEADS])
        kmax = sb("kmax", [P, K2, U])
        nkmax = sb("nkmax", [P, K2])
        nkrow = sb("nkrow", [1, K2, P])
        ctx_t = sb("ctx_t", [P, K2, P])
        ksum_r = sb("ksum_r", [P, K2])
        mix_w = sb("mix_w", [P, K2, D])
        h1t = sb("h1t", [P, 2, K2, U])
        h2t = sb("h2t", [P, 2, U])
        t3t = sb("t3t", [P, 2, K2, U])
        e1t = sb("e1t", [P, 2, NE, U])
        e2t = sb("e2t", [P, 2, NE // 2, U])
        e2g = sb("e2g", [P, 2, NE // 2, U])
        g5 = sb("g5", [P, 2, NE + 1])
        g5t = sb("g5t", [NE + 1, 2, U])
        gs = sb("gs", [P, 2, 8, NE])
        gsq = sb("gsq", [P, 2, 3, NE, NE])

        sort_a = sb("sort_a", [P, COLS])
        sort_b = sb("sort_b", [P, COLS])
        agg = sb("agg", [P, K2, WIDE])
        gath = sb("gath", [P, RING, D])
        hot = sb("hot", [P, RING, P])
        src_s = sort_b[:, 0:ECOLS].bitcast(I32)
        dst_s = sort_b[:, ECOLS:2 * ECOLS].bitcast(I32)
        node_s = sort_b[:, 2 * ECOLS:2 * ECOLS + NCOLS].bitcast(I32)
        row_f = sb("row_f", [P, COLS])
        wgt = sb("wgt", [P, COLS])
        typ_s = row_f[:, 0:ECOLS].bitcast(I32)
        mid_s = row_f[:, ECOLS:2 * ECOLS].bitcast(I32)
        x_all = agg[:].rearrange("p k n -> p (k n)").rearrange("p (u d) -> p u d", d=D)
        gath_flat = gath[:].rearrange("p r d -> p (r d)")
        xnt_ring = gath_flat[:, 0:CHUNK * K2 * U].rearrange("p (m k n) -> p m k n", m=CHUNK, k=K2)
        stats_all = sb("stats_all", [P, UNITS, 6])
        mean_all = sb("mean_all", [P, UNITS])
        var_all = sb("var_all", [P, UNITS])
        dif_all = sb("dif_all", [P, UNITS])
        rstd_all = sb("rstd_all", [P, UNITS])
        tile_min = sb("tile_min", [P, COLS // P])
        parts = sb("parts", [P, R, WCOLS])
        first = sb("first", [1, COLS], I32)
        cols = sb("cols", [P, RING], I32)
        half_row = sb("half_row", [1, 2 * BODIES + 1], I32)
        span = sb("span", [1, 2 * BODIES])
        body_info = sb("body_info", [1, BODIES, 4], I32)

        s_w = sem("weights_loaded")
        s_e = sem("edges_loaded")
        s_const = sem("constants_made")
        s_constv = sem("constants_made_dve")
        s_v = sem("dve_order")
        s_pl = sem("pool_order")
        s_xl = [sem(f"x_loaded{s}") for s in range(2)]
        s_tl = sem("xt_pair_loaded")
        s_stored = [sem(f"stored{s}") for s in range(2)]
        s_tstored = [sem(f"t_stored{s}") for s in range(2)]

        f_order = sem("final_order")
        s_x = [sem(f"x_loaded_chunk{c}") for c in range(CHUNKS)]
        n_var, n_rstd, n_xn, n_cp, n_tr, n_trc, n_kt, n_kmax, n_store, n_tstore0, n_tstore1, n_zero = (
            sem(n) for n in ("n_var", "n_rstd", "n_xn", "n_copied", "n_transposed", "n_xnt", "n_kt", "n_kmax",
                             "n_xn_stored", "n_xnt_stored0", "n_xnt_stored1", "n_agg_zeroed"))
        n_tstore = [n_tstore0, n_tstore1]
        b_ld = [sem(f"b_x_loaded{s}") for s in range(2)]
        b_st = [sem(f"b_xb_stored{s}") for s in range(2)]
        b_sum = sem("b_xb")
        s_order = {e: sem(f"{e}_order") for e in ("sp", "act", "pe")}
        m_neg, m_row, m_rowc = (sem(n) for n in ("neg_kmax", "neg_kmax_row", "neg_kmax_row_copied"))
        c_kv, c_exp, c_v, c_ctx, c_end = (sem(n) for n in ("c_kv", "c_kexp", "c_v", "c_context", "c_context_ended"))
        w_ctx, w_mm, w_done = (sem(n) for n in ("w_context_copied", "w_product", "mix_w_ready"))
        q_q, q_sub, q_exp, q_norm, q_tr, q_trc, q_o, q_var, q_rstd, q_ln, q_base = (sem(n) for n in (
            "q_q", "q_shifted", "q_exp", "q_softmax", "q_transposed", "q_t", "q_mix", "q_var", "q_rstd",
            "q_layernorm", "q_base"))
        r_rows, r_turn, r_min, r_line = (sem(n) for n in ("rows_ready", "rows_turned", "tile_minima", "minima_in_line"))
        s_turn, s_eva, s_key = sem("sort_blocks_turned"), sem("sort_blocks_copied"), sem("sort_turn_wanted")
        g_idx, g_mm, g_hot, g_acc = (sem(n) for n in ("columns_ready", "tile_summed", "one_hot", "accumulated"))
        g_in = [sem(f"gathered{j}") for j in range(RING)]
        f_ag, f_y, f_var, f_rstd, f_zn, f_tr, f_znt, f_h, f_relu, f_2, f_h2, f_e2, f_log, f_gl, f_ge = (
            sem(n) for n in ("f_agg", "f_y", "f_var", "f_rstd", "f_zn", "f_turned", "f_znt", "f_layer1",
                             "f_relu1", "f_layer2", "f_relu2s", "f_relu2e", "f_logits", "f_gatelogits", "f_gateexp"))
        f_keep, f_gate_order = sem("f_residual_kept"), sem("f_gate_order")
        f_p, f_pe, f_g, f_gt, f_gtc, f_gb, f_e2g, f_o, f_res = (sem(n) for n in (
            "f_gates", "f_gatesexp", "f_weights", "f_weights_turned", "f_weights_t", "f_spread", "f_gated",
            "f_out", "f_result"))

        turns, at_, plain = [], 0, [[(512 * q, 512 * q + 512, 1.0)] for q in range(4)]
        for k in range(8, BITS + 1):
            at_ = 1 - at_
            turns.append((at_, plain))
            at_ = (at_ + k - 7 + 1) % 2
            if k == BITS:
                break
            if k < 14:
                signs = [[(512 * q, 512 * q + 512, sign[:, k - 7:k - 6])] for q in range(4)]
            else:
                signs = [[(P * c, P * c + P, -1.0 if c >> (k - 14) & 1 else 1.0) for c in range(4 * q, 4 * q + 4)]
                         for q in range(4)]
            turns.append((at_, signs))
            at_ = (at_ + 7) % 2

        block = ctx.enter_context(nc.Block())
        NW = 20

        @block.sync
        def _(sp):
            for to, fro in ((src_s, src), (dst_s, dst), (typ_s, edge_type)):
                sp.dma_start(to[0:U], fro.rearrange("(p n) -> p n", p=U)).then_inc(s_e, 16)
            for c in range(CHUNKS):
                sp.dma_start(x_all[0:U, CHUNK * c:CHUNK * c + CHUNK, :],
                             x.rearrange("(u p) d -> p u d", p=U)[:, CHUNK * c:CHUNK * c + CHUNK, :]
                             ).then_inc(s_x[c], 16)
            loads = [
                (wqkv_s[:], wqkv.rearrange("(k p) n -> p k n", p=P)),
                (wout_s[:], wout.rearrange("(k p) n -> p k n", p=P)),
                (gnnw_s[:], gnn_w.rearrange("(k p) n -> p k n", p=P)),
                (sw1_s[:], sw1.rearrange("(k p) n -> p k n", p=P)),
                (sw2_s[:], sw2.rearrange("(k p) n -> p k n", p=P)),
                (sw3_s[:], sw3),
                (ew1_s[:, 0], ew1[:, 0:P].rearrange("e p h -> p e h")),
                (ew1_s[:, 1], ew1[:, P:2 * P].rearrange("e p h -> p e h")),
                (ew2_s[:], ew2.rearrange("e p h -> p e h")),
                (ew3_s[:], ew3.rearrange("(q h) g o -> (h g) q o", h=2)),
                (gw_s[:], gw.rearrange("(k p) n -> p k n", p=P)),
                (sb1_s[:], sb1.rearrange("(k p) -> p k", p=P)),
                (sb2_s[:], sb2.rearrange("(p a) -> p a", a=1)),
                (eb1_s[:], eb1.rearrange("e p -> p e")),
                (eb2_s[:], eb2.rearrange("(q h) g -> (h g) q", h=2)),
                (b5_s[0:NE], eb3),
                (b5_s[NE:NE + 1], sb3.rearrange("(a d) -> a d", a=1)),
                (gamma_b[:], gamma.rearrange("(a d) -> a d", a=1).to_broadcast([P, D])),
                (gnnb_b[:], gnn_b.rearrange("(a d) -> a d", a=1).to_broadcast([P, D])),
                (alpha_b[:], alpha.rearrange("r a -> a r").to_broadcast([P, R])),
                (gb_b[:], gb.rearrange("(a d) -> a d", a=1).to_broadcast([P, NE])),
            ]
            assert len(loads) == NW + 1
            for to, fro in loads:
                sp.dma_start(to, fro).then_inc(s_w, 16)

            def rows_of(u):
                return u * U if isinstance(u, int) else sp.snap(u * U)

            t = Tally(sp, s_order["sp"])
            def p1(c, warm):
                at = c * CHUNK if not warm else sp.snap(c * CHUNK)
                at5 = c * CHUNK + GROUP if not warm else sp.snap(c * CHUNK + GROUP)
                for g, a in ((0, at), (1, at5)):
                    sp.wait_ge(n_trc, c * CHUNK + GROUP * (g + 1))
                    sp.dma_start(xnt_dram[:, bass.ds(a, GROUP), :],
                                 xnt_ring[:, GROUP * g:GROUP * g + GROUP].rearrange("p m k n -> p m (k n)")
                                 ).then_inc(n_tstore[g], 16)
                sp.wait_ge(n_xn, c * CHUNK + CHUNK)
                sp.dma_start(xn_dram.rearrange("(u p) d -> p u d", p=U)[:, bass.ds(at, CHUNK), :],
                             x_all[0:U, bass.ds(at, CHUNK), :]).then_inc(n_store, 16)
            repeat(sp, t, p1, 0, CHUNKS)

            def xb(b, warm):
                at = [rows_of(2 * b + s) for s in range(2)]
                for s in range(2):
                    if warm:
                        sp.wait_ge(b_sum, 2 * b + s - 1)
                    sp.dma_start(xin[0:U, s], x[bass.ds(at[s], U), :]).then_inc(b_ld[s], 16)
                for s in range(2):
                    sp.wait_ge(b_sum, 2 * b + s + 1)
                    sp.dma_start(xb_dram[bass.ds(at[s], U), :], t2[0:U, s]).then_inc(b_st[s], 16)
            repeat(sp, t, xb, 0, PAIRS)
            for s in range(2):
                sp.wait_ge(n_tstore[s], 16 * CHUNKS)
                sp.wait_ge(b_st[s], 16 * PAIRS)

            def load_xnt(b, freed, count):
                at = 2 * b if isinstance(b, int) else sp.snap(2 * b)
                if count is not None:
                    sp.wait_ge(freed, count)
                sp.dma_start(xnt[:].rearrange("p s k n -> p s (k n)"),
                             xnt_dram[:, bass.ds(at, 2), :]).then_inc(s_tl, 16)

            def p2(b, warm):
                load_xnt(b, c_kv, 2 * b if warm else None)
            repeat(sp, t, p2, 0, PAIRS)

            def load_x(b):
                at = [rows_of(2 * b + s) for s in range(2)]
                for s in range(2):
                    sp.dma_start(xin[0:U, s], xb_dram[bass.ds(at[s], U), :]).then_inc(s_xl[s], 16)

            def store_base(b):
                at = [rows_of(2 * b + s) for s in range(2)]
                for s in range(2):
                    sp.wait_ge(q_base, 2 * b + s + 1)
                    sp.dma_start(base_dram[bass.ds(at[s], U), :], t2[0:U, s]).then_inc(s_stored[s], 16)

            load_xnt(0, c_kv, UNITS)
            load_x(0)
            load_xnt(1, q_q, 2)
            load_xnt(2, q_q, 4)

            def p3(b, warm):
                if not isinstance(b, int) or b < PAIRS - 1:
                    load_xnt(b + 1, q_q, 2 * b + 2)
                store_base(b - 2)
                load_x(b - 1)
            repeat(sp, t, p3, 2, PAIRS - 1)
            p3(PAIRS - 1, True)
            store_base(PAIRS - 2)
            load_x(PAIRS - 1)
            store_base(PAIRS - 1)
            for s in range(2):
                sp.wait_ge(s_stored[s], 16 * PAIRS)

            sp.wait_ge(g_idx, 2)
            final = FinalUnits(sp, U, UNITS)

            def load_base(n):
                at = sp.snap(n * U)
                sp.wait_ge(q_base, n + UNITS)
                sp.dma_start(xin[0:U, 0], base_dram[bass.ds(at, U), :]).then_inc(s_xl[0], 16)
                final.begin()
            with sp.Fori(2 * PAIRS + 1, BODIES) as i:
                with final.due(load_info(nc, sp, body_info, i, N, 1)):
                    n = final.next()
                    load_base(n)
            final.run_left(load_base)
            sp.wait_ge(s_stored[0], 16 * PAIRS + 16 * UNITS)

        @block.gpsimd
        def _(pool):
            t = Tally(pool, s_pl)
            t.mark(pool.memset(ident[:], 0.0))
            t.mark(pool.memset(ones[:], 1.0))
            t.mark(pool.memset(half_pow[:], -0.5))
            pool.memset(zeros[:], 0.0).then_inc(s_const, 1)
            t.mark(pool.memset(g5[:], 1.0))
            t.mark(pool.memset(before[:], 1.0))
            t.settle()
            pool.affine_select(out=ident[:], in_=ident[:], compare_op=ALU.not_equal, fill=1.0, base=0,
                               pattern=[[-1, P]], channel_multiplier=1).then_inc(s_const, 1)
            pool.affine_select(out=before[:], in_=before[:], compare_op=ALU.is_gt, fill=0.0, base=0,
                               pattern=[[1, NE], [-1, NE]], channel_multiplier=0).then_inc(s_const, 1)
            pool.iota(iota_p[:], [[0, 1]], base=0, channel_multiplier=1).then_inc(s_const, 1)
            pool.iota(expert_i[:], [[2, 2], [1, 2], [0, EH2]], base=0, channel_multiplier=-1).then_inc(s_const, 1)
            pool.iota(node_s[0:U], [[1, NCOLS]], base=0, channel_multiplier=NCOLS).then_inc(s_const, 1)
            pool.iota(nodes[:], [[1, WIDE]], base=0, channel_multiplier=0,
                      allow_small_or_imprecise_dtypes=True).then_inc(s_const, 1)

            pool.wait_ge(n_var, 1)
            pool.tensor_tensor(rstd_all[0:U], var_all[0:U], half_pow[0:U].to_broadcast([U, UNITS]),
                               ALU.pow).then_inc(n_rstd, 1)

            pool.wait_ge(s_w, 16 * (NW + 1))

            def xb(b, warm):
                for s in range(2):
                    if warm:
                        pool.wait_ge(b_st[s], 16 * b)
                    pool.wait_ge(b_ld[s], 16 * b + 16)
                    pool.tensor_tensor(t2[0:U, s], xin[0:U, s], gnnb_b[0:U], ALU.add).then_inc(b_sum, 1)
            repeat(pool, t, xb, 0, PAIRS)

            pool.wait_ge(n_store, 16 * CHUNKS)
            pool.wait_ge(n_cp, UNITS)
            pool.memset(agg[:], 0.0).then_inc(n_zero, 1)
            for s in range(2):
                pool.wait_ge(n_tstore[s], 16 * CHUNKS)
            pool.wait_ge(n_kt, UNITS)

            def gathers(i, warm):
                for j in range(RING):
                    if j % HALF == 0:
                        t.settle()
                        pool.wait_ge(g_idx, 2 * i + j // HALF + 1)
                        t.mark(pool.tensor_tensor(carrier[0:1], half_pow[0:1], half_pow[0:1], ALU.add))
                    pool.indirect_dma_start(gath[:, j], None, xn_dram[:, :],
                                            bass.IndirectOffsetOnAxis(ap=cols[:, j:j + 1], axis=0)).then_inc(g_in[j], 16)
            repeat(pool, t, gathers, 0, BODIES)

        @block.scalar
        def _(act):
            act.wait_ge(s_const, 7)
            act.wait_ge(s_w, 16 * (NW + 1))

            t = Tally(act, s_order["act"])

            def p1(c, warm):
                for m in range(CHUNK + 1):
                    u = c * CHUNK + m
                    if m < CHUNK:
                        act.wait_ge(n_xn, u + 1)
                        if warm or m >= 2:
                            act.wait_ge(n_tr, u - 1)
                        act.copy(t0[0:U, m % 2], x_all[0:U, bass.ds(u, 1), :].rearrange("p a d -> p (a d)")
                                 ).then_inc(n_cp, 1)
                    if m >= 1:
                        act.wait_ge(n_tr, u)
                        if warm and m == 1:
                            act.wait_ge(n_tstore[0], 16 * c)
                            act.wait_ge(n_kt, c * CHUNK)
                        if warm and m == GROUP + 1:
                            act.wait_ge(n_tstore[1], 16 * c)
                        act.copy(xnt_ring[:, m - 1], bank[(m - 1) % 2][:, 0:K2 * U].rearrange("p (k n) -> p k n", k=K2)
                                 ).then_inc(n_trc, 1)
            repeat(act, t, p1, 0, CHUNKS)
            act.wait_ge(m_row, 1)
            act.copy(nkrow[:], bank[2][0:1, 0:D].rearrange("p (k n) -> p k n", k=K2)).then_inc(m_rowc, 1)

            for n, (to, signs) in enumerate(turns):
                for q in (1, 3):
                    act.wait_ge(s_turn, 4 * n + q + 1)
                    for lo, hi, sc in signs[q]:
                        last = act.activation((sort_a, sort_b)[to][:, lo:hi], bank[q][:, lo - 512 * q:hi - 512 * q],
                                              ACT.Copy, scale=sc)
                    last.then_inc(s_eva, 1)

            def p2(b, warm):
                for s in range(2):
                    u = 2 * b + s
                    act.wait_ge(c_kv, u + 1)
                    if warm:
                        act.wait_ge(c_ctx, u - 1)
                    act.activation(t0[0:U, s], bank[4 + s][0:U, 0:D], ACT.Exp).then_inc(c_exp, 1)
                    act.copy(t1[0:U, s], bank[4 + s][0:U, D:2 * D]).then_inc(c_v, 1)
            repeat(act, t, p2, 0, PAIRS)

            def p3(b, warm):
                for s in range(2):
                    u = 2 * b + s
                    act.wait_ge(q_sub, u + 1)
                    if warm:
                        act.wait_ge(q_tr, u - 1)
                    for h in range(HEADS):
                        last = act.activation(t0[0:U, s, h * DH:(h + 1) * DH], bank[2 + s][0:U, h * DH:(h + 1) * DH],
                                              ACT.Exp, bias=head[0:U, s, 2, h:h + 1])
                    last.then_inc(q_exp, 1)
                for s in range(2):
                    u = 2 * b + s
                    act.wait_ge(q_tr, u + 1)
                    if warm:
                        act.wait_ge(q_o, u - 1)
                    act.copy(h1t[:, s], bank[4 + s][:, 0:K2 * U].rearrange("p (k n) -> p k n", k=K2)).then_inc(q_trc, 1)
            repeat(act, t, p3, 0, PAIRS)

            final = FinalUnits(act, U, UNITS)

            def weights_out(n):
                act.wait_ge(f_gt, n)
                act.copy(g5t[:, 0], bank[2][0:NE + 1, 0:U]).then_inc(f_gtc, 1)

            def result_out(n):
                at = n * U - U if isinstance(n, int) else act.snap(nc.s_assert_within(n * U - U, 0, N - U))
                act.wait_ge(f_res, n)
                act.dma_start(out[bass.ds(at, U), :], t2[0:U, 0]).then_inc(s_stored[0], 16)

            def gate_part(n):
                act.wait_ge(f_zn, n)
                act.copy(t1[0:U, 1], t1[0:U, 0]).then_inc(f_keep, 1)
                act.wait_ge(f_gl, n)
                act.activation(gs[0:U, 0, 1], gs[0:U, 0, 0], ACT.Exp).then_inc(f_ge, 1)
                act.wait_ge(f_p, n)
                act.activation(gs[0:U, 0, 4], gs[0:U, 0, 3], ACT.Exp).then_inc(f_pe, 1)
                act.wait_ge(f_h, n)
                for k in range(K2):
                    act.activation(h1t[:, 0, k], bank[5][:, k * U:k * U + U], ACT.Relu, bias=sb1_s[:, k:k + 1])
                for e in range(NE):
                    last = act.activation(e1t[:, 0, e], bank[6][:, e * U:e * U + U], ACT.Relu, bias=eb1_s[:, e:e + 1])
                last.then_inc(f_relu, 1)
                weights_out(n)
                act.wait_ge(f_2, n)
                act.activation(h2t[:, 0], bank[5][:, D:D + U], ACT.Relu, bias=sb2_s[:, 0:1]).then_inc(f_h2, 1)

            def unit(acc, n):
                act.wait_ge(g_acc, acc)
                act.copy(xnt[:, 0], agg[:, :, bass.ds(n * U, U)]).then_inc(f_ag, 1)
                with act.If(n > 0):
                    gate_part(n)
                act.wait_ge(f_tr, n + 1)
                act.copy(t3t[:, 0], bank[4][:, D:D + K2 * U].rearrange("p (k n) -> p k n", k=K2)).then_inc(f_znt, 1)
                with act.If(n > 0):
                    result_out(n)
                final.begin()
            for s in range(2):
                act.wait_ge(s_stored[s], 16 * PAIRS)
            with act.Fori(2 * PAIRS + 1, BODIES) as i:
                with final.due(load_info(nc, act, body_info, i, N, 1)):
                    n = final.next()
                    unit(BODY_ACC * i - HALF_ACC, n)
            final.run_left(lambda n: unit(BODY_ACC * BODIES, n))
            gate_part(UNITS)
            result_out(UNITS)

        @block.vector
        def _(dve):
            t = Tally(dve, s_v)

            def do(ins):
                t.mark(ins)
                t.settle()

            V = nc.vector
            dve.wait_ge(s_const, 6)
            for b in range(7):
                t.mark(V.tensor_scalar(bit_i[:, b:b + 1], iota_p[:], b, 1, ALU.logical_shift_right, ALU.bitwise_and))
            t.mark(V.memset(kmax[:], -3.0e38))
            t.mark(V.tensor_scalar(spread[:].rearrange("e q p -> e (q p)"),
                                   expert_i[:].rearrange("e q h g -> e (q h g)"), 0.0, None, ALU.is_equal))
            t.settle()
            do(V.tensor_scalar(sign[:], bit_i[:], -2.0, 1.0, ALU.mult, ALU.add))
            V.memset(ctx_t[:], 0.0).then_inc(s_constv, 1)

            dve.wait_ge(s_e, 48)
            A, B = sort_a, sort_b
            Ai, Bi = A[:].bitcast(I32), B[:].bitcast(I32)
            pad = BIAS | PAD_ROW << ROW_SHIFT | R
            t.mark(V.memset(Ai, pad))
            do(V.tensor_scalar(typ_s[0:U], typ_s[0:U], BIAS, None, ALU.bitwise_or))
            for row, col, c0 in ((src_s, dst_s, 0), (dst_s, src_s, ECOLS)):
                do(V.tensor_scalar(mid_s[0:U], col[0:U], COL_SHIFT, None, ALU.logical_shift_left))
                do(V.tensor_tensor(mid_s[0:U], mid_s[0:U], typ_s[0:U], ALU.bitwise_or))
                do(V.tensor_scalar(Ai[0:U, c0:c0 + ECOLS], row[0:U], ROW_SHIFT, None, ALU.logical_shift_left))
                do(V.tensor_tensor(Ai[0:U, c0:c0 + ECOLS], Ai[0:U, c0:c0 + ECOLS], mid_s[0:U], ALU.bitwise_or))
            own = Ai[0:U, 2 * ECOLS:2 * ECOLS + NCOLS]
            do(V.tensor_scalar(own, node_s[0:U], ROW_SHIFT, BIAS | R, ALU.logical_shift_left, ALU.bitwise_or))
            do(V.tensor_scalar(node_s[0:U], node_s[0:U], COL_SHIFT, None, ALU.logical_shift_left))
            do(V.tensor_tensor(own, own, node_s[0:U], ALU.bitwise_or))
            do(V.tensor_scalar(A[:], A[:], sign[:, 0:1], None, ALU.mult))

            buf = [A, B]
            at = 0
            nready = 0

            def compare(j, k, negated=False, ready=False):
                nonlocal at, nready
                todo = []
                parts_of = [slice(0, COLS)]
                if ready:
                    parts_of = [slice(0, COLS // 2), slice(COLS // 2, COLS)]

                def pick(y, x0, x1, op):
                    todo.append((y, x0, x1, op))
                i = 1 << j
                if k is not None and ready and 1 << (k + 1) == COLS:
                    parts_of = [slice(0, COLS)]
                for part in parts_of:
                    a, o = buf[at][:, part], buf[1 - at][:, part]
                    if k is None:
                        va, vo = (z.rearrange("p (o t i) -> p o t i", t=2, i=i) for z in (a, o))
                        pick(vo[:, :, 0], va[:, :, 0], va[:, :, 1], ALU.min)
                        pick(vo[:, :, 1], va[:, :, 0], va[:, :, 1], ALU.max)
                        continue
                    m = 1 << (k - j - 1)
                    va, vo = (z.rearrange("p (o d m t i) -> p o d m t i", d=2, m=m, t=2, i=i) for z in (a, o))
                    for d in range(2):
                        for lo in range(2):
                            op = ALU.min if lo == d else ALU.max
                            mid = 0 if m == 1 else slice(0, m)
                            pick(vo[:, :, d, mid, lo], va[:, :, d, mid, 0], va[:, :, d, mid, 1], op)
                for n, (y, x0, x1, op) in enumerate(todo):
                    if negated:
                        ins = V.scalar_tensor_tensor(y, x1, -1.0, x0, ALU.mult, op)
                    else:
                        ins = V.tensor_tensor(y, x0, x1, op)
                    if ready and n + 1 in (len(todo) // 2, len(todo)):
                        ins.then_inc(s_key, 1)
                        nready += 1
                        if n + 1 == len(todo):
                            dve.wait_ge(s_key, nready)
                    else:
                        t.mark(ins)
                t.settle()
                at = 1 - at

            nturn = 0

            def turn():
                nonlocal at, nturn
                signs = turns[nturn][1]
                for q in (0, 2):
                    dve.wait_ge(s_turn, 4 * nturn + q + 1)
                    for lo, hi, sc in signs[q]:
                        t.mark(V.tensor_scalar(buf[1 - at][:, lo:hi], bank[q][:, lo - 512 * q:hi - 512 * q], sc, None,
                                               ALU.mult))
                t.settle()
                nturn += 1
                dve.wait_ge(s_eva, 2 * nturn)
                at = 1 - at

            for k in range(1, 8):
                for j in range(k - 1, -1, -1):
                    compare(j, k if k < 7 else None, ready=(k == 7 and j == 0))
            for c in range(CHUNKS):
                dve.wait_ge(s_x[c], 16)
            with dve.Fori(0, CHUNKS) as c:
                for m in range(CHUNK):
                    u = c * CHUNK + m
                    V.bn_stats(stats_all[0:U, bass.ds(u, 1)].rearrange("p a d -> p (a d)"),
                               x_all[0:U, bass.ds(u, 1)].rearrange("p a d -> p (a d)")).then_inc(n_stat, 1)
            dve.wait_ge(n_stat, UNITS)
            st = stats_all[0:U]
            mean_e, m2_e, mean_o, m2_o = st[:, :, 1], st[:, :, 2], st[:, :, 4], st[:, :, 5]
            mean, var, dif = mean_all[0:U], var_all[0:U], dif_all[0:U]
            t.mark(V.tensor_tensor(mean, mean_e, mean_o, ALU.add))
            t.mark(V.tensor_tensor(dif, mean_e, mean_o, ALU.subtract))
            do(V.tensor_tensor(var, m2_e, m2_o, ALU.add))
            t.mark(V.tensor_scalar(mean, mean, 0.5, None, ALU.mult))
            do(V.scalar_tensor_tensor(dif, dif, 0.25, dif, ALU.mult, ALU.mult))
            do(V.scalar_tensor_tensor(var, var, 1.0 / D, dif, ALU.mult, ALU.add))
            V.tensor_scalar(var, var, EPS, None, ALU.add).then_inc(n_var, 1)
            dve.wait_ge(n_rstd, 1)
            KLAG = 4

            def p1(c, warm):
                for m in range(CHUNK + KLAG):
                    u = c * CHUNK + m
                    if m < CHUNK:
                        xu = x_all[0:U, bass.ds(u, 1)].rearrange("p a d -> p (a d)")
                        V.tensor_scalar(xu, xu, mean_all[0:U, bass.ds(u, 1)], rstd_all[0:U, bass.ds(u, 1)],
                                        ALU.subtract, ALU.mult).then_inc(n_xn, 1)
                    if m >= KLAG:
                        dve.wait_ge(n_kt, u - KLAG + 1)
                        dve.wait_ge(n_kmax, u - KLAG)
                        V.tensor_tensor(kmax[:], bank[3 + (m - KLAG) % 5][:, 0:K2 * U].rearrange("p (k n) -> p k n", k=K2),
                                        kmax[:], ALU.max).then_inc(n_kmax, 1)
            repeat(dve, t, p1, 0, CHUNKS)
            dve.wait_ge(n_kmax, UNITS)
            do(V.tensor_reduce(nkmax[:], kmax[:], AX.X, ALU.max))
            V.tensor_scalar(nkmax[:], nkmax[:], -1.0, None, ALU.mult).then_inc(m_neg, 1)

            for k in range(8, BITS + 1):
                turn()
                for j in range(k - 1, 6, -1):
                    compare(j - 7, None if k == BITS else k - 7, negated=(j == k - 1), ready=(j == 7 and k < BITS))
                if k == BITS:
                    break
                turn()
                for j in range(6, -1, -1):
                    compare(j, None, ready=(j == 0))
            assert nturn == len(turns)
            S, T = buf[at], buf[1 - at]
            Si, Ti = S[:].bitcast(I32), T[:].bitcast(I32)

            do(V.tensor_scalar(Ti, Si, ROW_SHIFT, ID_MASK, ALU.logical_shift_right, ALU.bitwise_and))
            V.tensor_copy(row_f[:], Ti).then_inc(r_rows, 1)
            dve.wait_ge(r_rows, 1)
            t.mark(V.tensor_scalar(Ti, Si, REL_MASK, None, ALU.bitwise_and))
            for q in range(4):
                dve.wait_ge(r_turn, q + 1)
                V.tensor_reduce(tile_min[:, 4 * q:4 * q + 4], bank[q][:].rearrange("p (c m) -> p c m", m=P), AX.X,
                                ALU.min).then_inc(r_min, 1)
            for q in range(4):
                dve.wait_ge(r_line, q + 1)
                t.mark(V.tensor_scalar(first[:, 512 * q:512 * q + 512], bank[4 + q][0:1], float(N - 1), None, ALU.min))
            t.settle()
            do(V.tensor_copy(half_row[:], first[:, 0:TILE_END:HALF]))
            do(V.tensor_tensor(span[:], half_row[:, 1:2 * BODIES + 1], half_row[:, 0:2 * BODIES], ALU.subtract))
            pairs = span[:].rearrange("o (b h) -> o b h", h=2)
            do(V.tensor_tensor(pairs[:, :, 0], pairs[:, :, 0], pairs[:, :, 1], ALU.max))
            t.mark(V.tensor_scalar(body_info[:, :, 3], pairs[:, :, 0], float(WINDOW), None, ALU.is_ge))
            t.mark(V.memset(body_info[:, 0, 0:1], 0.0))
            for c in range(3):
                b0 = 1 if c == 0 else 0
                t.mark(V.tensor_copy(body_info[:, b0:BODIES, c],
                                     half_row[:, 2 * b0 + c - 1:2 * BODIES + c - 2:2]))
            t.settle()
            dve.wait_ge(s_const, 7)
            dve.wait_ge(s_w, 16 * (NW + 1))
            dve.wait_ge(n_zero, 1)
            for s in range(2):
                dve.wait_ge(n_tstore[s], 16 * CHUNKS)

            def weights(at):
                t.settle()
                for r in range(R):
                    t.mark(V.tensor_scalar(parts[:, r], Ti[:, bass.ds(at, WCOLS)], float(r), alpha_b[:, r:r + 1],
                                           ALU.is_equal, ALU.mult))
                t.settle()
                t.mark(V.tensor_reduce(wgt[:, bass.ds(at, WCOLS)], parts[:].rearrange("p r c -> p c r"), AX.X, ALU.add))

            def unpack_cols(tile0, j0):
                V.tensor_scalar(cols[:, j0:j0 + HALF], Si[:, bass.ds(tile0, HALF)], COL_SHIFT, ID_MASK,
                                ALU.logical_shift_right, ALU.bitwise_and).then_inc(g_idx, 1)
            unpack_cols(0, 0)
            unpack_cols(HALF, HALF)
            weights(0)
            t.settle()

            def rows_from(table, at, count):
                _, vals = nc.values_load_multi_w_load_instructions(
                    table[0:1, bass.ds(at, count)], engines=[dve.engine], min_val=0, max_val=N - 1,
                    skip_runtime_bounds_check_because="clamped to the last node when unpacked, and rows are not negative")
                return vals

            def one_hot(i, j, r0, width):
                tile = RING * i + j
                V.tensor_scalar(hot[:, j, 0:width], nodes[:, bass.ds(r0, width)], row_f[:, bass.ds(tile, 1)],
                                wgt[:, bass.ds(tile, 1)], ALU.is_equal, ALU.mult).then_inc(g_hot, 1)

            def add_window(b, r0, width):
                window = agg[:, :, bass.ds(r0, width)]
                return V.tensor_tensor(window, bank[b][:, 0:K2 * width].rearrange("p (k n) -> p k n", k=K2), window,
                                       ALU.add)

            def accumulate_half(i, half, r0):
                dve.wait_ge(g_mm, RING * i + HALF * (half + 1))
                if half or not isinstance(i, int) or i > 0:
                    dve.wait_ge(g_acc, BODY_ACC * i + HALF_ACC * half)
                add_window(half, r0, WINDOW).then_inc(g_acc, HALF_ACC)

            def narrow_body(i, started, beside, rows):
                for j in range(RING):
                    if j == HOT_AHEAD and started:
                        accumulate_half(i - 1, 1, rows[0])
                        unpack_cols(RING * i + HALF, HALF)
                    if j == HALF + HOT_AHEAD:
                        accumulate_half(i, 0, rows[1])
                        unpack_cols(RING * i + RING, 0)
                    one_hot(i, j, rows[2] if j >= HALF else rows[1], WINDOW)
                    if j in beside:
                        beside[j]()

            def wide_body(i, started, beside, info):
                if started:
                    accumulate_half(i - 1, 1, info[0])
                    unpack_cols(RING * i + HALF, HALF)
                for q in range(0, RING, 4):
                    rows = rows_from(first, RING * i + q, 4)
                    for j in range(q, q + 4):
                        one_hot(i, j, rows[j - q], P)
                        dve.wait_ge(g_mm, RING * i + j + 1)
                        if j or started:
                            dve.wait_ge(g_acc, BODY_ACC * i + j)
                        add_window(j % 2, rows[j - q], P).then_inc(g_acc, 1)
                        if j == HALF - 1:
                            unpack_cols(RING * i + RING, 0)
                dve.wait_ge(g_acc, BODY_ACC * i + RING)
                V.memset(bank[1][:, 0:K2 * WINDOW], 0.0).then_inc(g_acc, 1)
                for j in sorted(beside):
                    beside[j]()

            def gather_body(i, started, beside, tallies, info=None):
                info = info or load_info(nc, dve, body_info, i, N, 4)
                either(dve, tallies, info[3] < 1, lambda: narrow_body(i, started, beside, info),
                       lambda: wide_body(i, started, beside, info))

            repeat(dve, t, lambda i, warm: gather_body(i, warm, {12: lambda: weights(WCOLS * i + WCOLS)}, [t]), 0,
                   PAIRS)

            dve.wait_ge(c_end, K2)
            for h in range(HEADS):
                k, p0 = h // 4, DH * (h % 4)
                t.mark(V.tensor_copy(ctx_t[p0:p0 + DH, k, p0:p0 + DH], bank[6 + k][p0:p0 + DH, h * DH:(h + 1) * DH]))
            for k in range(K2):
                t.mark(V.reciprocal(ksum_r[:, k:k + 1], bank[6 + k][:, D:D + 1]))
            t.settle()
            V.tensor_scalar(ksum_r[:], ksum_r[:], SCALE, None, ALU.mult).then_inc(w_ctx, 1)
            dve.wait_ge(w_ctx, 1)
            dve.wait_ge(w_mm, 1)
            for k in range(K2):
                V.tensor_scalar(mix_w[:, k], bank[4][:, k * D:k * D + D], ksum_r[:, k:k + 1], None,
                                ALU.mult).then_inc(w_done, 1)

            def moments(t, units):
                def do(ins):
                    t.mark(ins)
                    t.settle()
                for q, unit in enumerate(units):
                    t.mark(V.bn_stats(stats[0:U, q], unit))
                t.settle()
                w = len(units)
                st = stats[0:U, 0:w]
                mean, var, dif = mv[0:U, 0:w, 0], mv[0:U, 0:w, 1], mdif[0:U, 0:w]
                t.mark(V.tensor_tensor(mean, st[:, :, 1], st[:, :, 4], ALU.add))
                t.mark(V.tensor_tensor(dif, st[:, :, 1], st[:, :, 4], ALU.subtract))
                do(V.tensor_tensor(var, st[:, :, 2], st[:, :, 5], ALU.add))
                t.mark(V.tensor_scalar(mean, mean, 0.5, None, ALU.mult))
                t.mark(V.tensor_scalar(var, var, 1.0 / D, EPS, ALU.mult, ALU.add))
                do(V.scalar_tensor_tensor(dif, dif, 0.25, dif, ALU.mult, ALU.mult))
                do(V.tensor_tensor(var, var, dif, ALU.add))
                y, a = rstd[0:U, 0:w, 0], newton[0:U, 0:w]
                do(V.tensor_scalar(y.bitcast(I32), var.bitcast(I32), 1, None, ALU.logical_shift_right))
                do(V.tensor_scalar(y.bitcast(I32), y.bitcast(I32), -1.0, float(0x5F3759DF), ALU.mult, ALU.add))
                for _ in range(3):
                    do(V.tensor_tensor(a, y, y, ALU.mult))
                    do(V.scalar_tensor_tensor(a, a, -0.5, var, ALU.mult, ALU.mult))
                    do(V.scalar_tensor_tensor(y, a, 1.5, y, ALU.add, ALU.mult))

            def mix_norm(b):
                for s in range(2):
                    dve.wait_ge(q_o, 2 * b + s + 1)
                moments(t, [bank[6][0:U, 0:D], bank[7][0:U, 0:D]])
                for s in range(2):
                    V.scalar_tensor_tensor(t1[0:U, s], bank[6 + s][0:U, 0:D], mv[0:U, s, 0:1], gamma_b[0:U],
                                           ALU.subtract, ALU.mult).then_inc(q_ln, 1)
                dve.wait_ge(q_ln, 2 * b + 2)
                for s in range(2):
                    dve.wait_ge(s_xl[s], 16 * b + 16)
                    dve.wait_ge(s_stored[s], 16 * b)
                    V.scalar_tensor_tensor(t2[0:U, s], t1[0:U, s], rstd[0:U, s], xin[0:U, s], ALU.mult,
                                           ALU.add).then_inc(q_base, 1)

            def p3_steps(b, warm):
                def heads_max():
                    for s in range(2):
                        q = bank[2 + s][0:U, 0:D].rearrange("p (h d) -> p h d", h=HEADS)
                        dve.wait_ge(q_q, 2 * b + s + 1)
                        t.mark(V.tensor_reduce(head[0:U, s, 0], q, AX.X, ALU.max))
                    t.settle()
                    for s in range(2):
                        V.tensor_scalar(head[0:U, s, 2], head[0:U, s, 0], -1.0, None, ALU.mult).then_inc(q_sub, 1)

                def heads_scale():
                    for s in range(2):
                        e = t0[0:U, s].rearrange("p (h d) -> p h d", h=HEADS)
                        dve.wait_ge(q_exp, 2 * b + s + 1)
                        do(V.tensor_reduce(head[0:U, s, 0], e, AX.X, ALU.add))
                        do(V.reciprocal(head[0:U, s, 1], head[0:U, s, 0]))
                        V.tensor_tensor(e, e, head[0:U, s, 1].unsqueeze(2).to_broadcast([U, HEADS, DH]),
                                        ALU.mult).then_inc(q_norm, 1)
                steps = {6: heads_max, 15: heads_scale}
                if warm:
                    steps[9] = lambda: mix_norm(b - 2)
                return steps

            gather_body(PAIRS, True, p3_steps(0, False), [t])
            gather_body(PAIRS + 1, True, p3_steps(1, False), [t])
            repeat(dve, t, lambda i, warm: gather_body(i, True, p3_steps(i - PAIRS, True), [t]), PAIRS + 2, 2 * PAIRS)
            gather_body(2 * PAIRS, True, {4: lambda: mix_norm(PAIRS - 2), 15: lambda: mix_norm(PAIRS - 1)}, [t])
            final = FinalUnits(dve, U, UNITS)
            f = Tally(dve, f_order)
            V.memset(carrier[64:65], 0.0).then_inc(f_keep, 1)
            HEAD_STEPS, GATE_STEPS = 19, 12
            fg = Tally(dve, f_gate_order)
            V.memset(carrier[96:97], 0.0).then_inc(f_gate_order, GATE_STEPS)

            def experts(n):
                dve.wait_ge(f_2, n)
                for q in range(NE // 2):
                    last = V.tensor_scalar(e2t[:, 0, q], bank[7][:, q * U:q * U + U], eb2_s[:, q:q + 1], 0.0,
                                           ALU.add, ALU.max)
                last.then_inc(f_e2, 1)
                dve.wait_ge(f_e2, n)
                dve.wait_ge(f_gb, n)
                V.tensor_tensor(e2g[:, 0], e2t[:, 0], bank[3][:, 0:2 * U].rearrange("p (q n) -> p q n", q=2),
                                ALU.mult).then_inc(f_e2g, 1)

            def result(n):
                dve.wait_ge(f_o, n)
                dve.wait_ge(f_keep, n + 1)
                dve.wait_ge(s_stored[0], n * 16 + (16 * PAIRS - 16))
                V.tensor_tensor(t2[0:U, 0], bank[2][0:U, D:2 * D], t1[0:U, 1], ALU.add).then_inc(f_res, 1)

            def residual(n):
                assert f.marks % HEAD_STEPS == 0
                f.count = n * HEAD_STEPS
                dve.wait_ge(f_keep, n + 1)
                dve.wait_ge(f_y, n + 1)
                dve.wait_ge(s_xl[0], n * 16 + (16 * PAIRS + 16))
                V.tensor_tensor(t1[0:U, 0], bank[4][0:U, 0:D], xin[0:U, 0], ALU.add).then_inc(q_base, 1)
                dve.wait_ge(q_base, n + (UNITS + 1))
                moments(f, [t1[0:U, 0]])
                V.tensor_scalar(t0[0:U, 0], t1[0:U, 0], mv[0:U, 0, 0:1], rstd[0:U, 0], ALU.subtract,
                                ALU.mult).then_inc(f_zn, 1)

            def gates(n):
                def do(ins):
                    fg.mark(ins)
                    fg.settle()
                assert fg.marks % GATE_STEPS == 0
                fg.count = n * GATE_STEPS
                g = gs[0:U, 0]
                h = head[0:U, 0, 0]
                dve.wait_ge(f_log, n)
                do(V.tensor_tensor(g[:, 0], bank[3][0:U, D:D + NE], gb_b[0:U], ALU.add))
                do(V.tensor_reduce(h[:, 0:1], g[:, 0], AX.X, ALU.max))
                V.tensor_scalar(g[:, 0], g[:, 0], h[:, 0:1], None, ALU.subtract).then_inc(f_gl, 1)
                dve.wait_ge(f_ge, n)
                do(V.tensor_reduce(h[:, 0:1], g[:, 1], AX.X, ALU.add))
                do(V.reciprocal(h[:, 1:2], h[:, 0:1]))
                V.tensor_scalar(g[:, 3], g[:, 1], h[:, 1:2], None, ALU.mult).then_inc(f_p, 1)
                dve.wait_ge(f_p, n)
                mine = g[:, 3].unsqueeze(2).to_broadcast([U, NE, NE])
                other = g[:, 3].unsqueeze(1).to_broadcast([U, NE, NE])
                sq = gsq[0:U, 0]
                fg.mark(V.tensor_tensor(sq[:, 0], other, mine, ALU.is_gt))
                do(V.tensor_tensor(sq[:, 1], other, mine, ALU.is_equal))
                do(V.tensor_tensor(sq[:, 1], sq[:, 1], before[0:U], ALU.mult))
                do(V.tensor_tensor(sq[:, 2], sq[:, 1], sq[:, 0], ALU.add))
                do(V.tensor_reduce(g[:, 5], sq[:, 2], AX.X, ALU.add))
                dve.wait_ge(f_pe, n)
                do(V.scalar_tensor_tensor(g[:, 6], g[:, 5], 1.5, g[:, 4], ALU.is_lt, ALU.mult))
                do(V.tensor_reduce(h[:, 2:3], g[:, 6], AX.X, ALU.add))
                do(V.reciprocal(h[:, 3:4], h[:, 2:3]))
                V.tensor_scalar(g5[0:U, 0, 0:NE], g[:, 6], h[:, 3:4], None, ALU.mult).then_inc(f_g, 1)

            def after_first(n, step):
                def run():
                    with dve.If(n > 0):
                        step(n)
                return run

            def unit_steps(n):
                return {4: after_first(n, gates), 8: lambda: residual(n), 9: after_first(n, experts),
                        15: after_first(n, result)}

            with dve.Fori(2 * PAIRS + 1, BODIES) as i:
                info = load_info(nc, dve, body_info, i, N, 4)
                with final.due(info):
                    n = final.next()
                    gather_body(i, True, unit_steps(n), [f, fg], info)
                    final.begin()
                with dve.Else():
                    gather_body(i, True, {}, [], info)
            accumulate_half(BODIES - 1, 1, rows_from(half_row, 2 * BODIES - 1, 1)[0])

            def rest(n):
                steps = unit_steps(n)
                for j in sorted(steps):
                    steps[j]()
                final.begin()
            final.run_left(rest)
            gates(UNITS)
            experts(UNITS)
            result(UNITS)

        @block.tensor
        def _(pe):
            M = nc.tensor.matmul
            pe.wait_ge(s_const, 7)
            pe.wait_ge(s_w, 16 * (NW + 1))

            def turn_unit(src_ap, s, to, o, done):
                for k in range(K2):
                    last = pe.transpose(to[:, o + k * U:o + k * U + U], src_ap[:, k * P:(k + 1) * P], ident[0:U, 0:U])
                last.then_inc(done, 1)

            t = Tally(pe, s_order["pe"])

            def p1(c, warm):
                for m in range(CHUNK + 1):
                    u = c * CHUNK + m
                    if m < CHUNK:
                        pe.wait_ge(n_cp, u + 1)
                        if warm or m >= 2:
                            pe.wait_ge(n_trc, u - 1)
                        turn_unit(t0[0:U, m % 2], 0, bank[m % 2], 0, n_tr)
                    if m >= 1:
                        pe.wait_ge(n_trc, u)
                        if warm or m >= 6:
                            pe.wait_ge(n_kmax, u - 5)
                        for f in range(K2):
                            for k in range(K2):
                                last = M(bank[3 + (m - 1) % 5][:, f * U:f * U + U],
                                         wqkv_s[:, k, D + f * P:D + f * P + P], xnt_ring[:, m - 1, k],
                                         start=(k == 0), stop=(k == K2 - 1))
                        last.then_inc(n_kt, 1)
            repeat(pe, t, p1, 0, CHUNKS)
            pe.wait_ge(m_neg, 1)
            for k in range(K2):
                last = pe.transpose(bank[2][0:1, k * P:(k + 1) * P], nkmax[:, k:k + 1], ident[:])
            last.then_inc(m_row, 1)
            pe.wait_ge(m_rowc, 1)

            for n, (to, _) in enumerate(turns):
                for q in range(4):
                    if q % 2 == 0:
                        pe.wait_ge(s_key, 2 * n + q // 2 + 1)
                    for c in range(4 * q, 4 * q + 4):
                        last = pe.transpose(bank[q][:, (c - 4 * q) * P:(c - 4 * q + 1) * P],
                                            (sort_a, sort_b)[1 - to][:, c * P:(c + 1) * P], ident[:])
                    last.then_inc(s_turn, 1)

            pe.wait_ge(r_rows, 1)
            for q in range(4):
                for c in range(4):
                    last = pe.transpose(bank[q][:, c * P:(c + 1) * P], row_f[:, (4 * q + c) * P:(4 * q + c + 1) * P],
                                        ident[:])
                last.then_inc(r_turn, 1)
            for q in range(4):
                pe.wait_ge(r_min, q + 1)
                for c in range(4):
                    last = pe.transpose(bank[4 + q][0:1, c * P:(c + 1) * P], tile_min[:, 4 * q + c:4 * q + c + 1],
                                        ident[:])
                last.then_inc(r_line, 1)

            def narrow_body(i, started, beside):
                for j in range(RING):
                    tile = RING * i + j
                    half = j // HALF
                    if j in beside:
                        beside[j]()
                    pe.wait_ge(g_in[j], 16 * i + 16)
                    pe.wait_ge(g_hot, tile + 1)
                    if j % HALF == 0 and started:
                        pe.wait_ge(g_acc, BODY_ACC * i - HALF_ACC * (1 - half))
                    elif j == 0:
                        pe.wait_ge(s_eva, 2 * len(turns))
                    for k in range(K2):
                        last = M(bank[half][:, k * WINDOW:(k + 1) * WINDOW], gath[:, j, k * P:(k + 1) * P],
                                 hot[:, j, 0:WINDOW], start=(j % HALF == 0 and k == 0), stop=(j % HALF == HALF - 1),
                                 skip_group_check=True)
                    if j % HALF == HALF - 1:
                        last.then_inc(g_mm, HALF)
                if RING in beside:
                    beside[RING]()

            def wide_body(i, started, beside):
                for j in range(RING):
                    tile = RING * i + j
                    pe.wait_ge(g_in[j], 16 * i + 16)
                    pe.wait_ge(g_hot, tile + 1)
                    if started or j >= 2:
                        pe.wait_ge(g_acc, BODY_ACC * i + max(j - 1, 0))
                    elif j == 0:
                        pe.wait_ge(s_eva, 2 * len(turns))
                    for k in range(K2):
                        last = M(bank[j % 2][:, k * P:(k + 1) * P], gath[:, j, k * P:(k + 1) * P], hot[:, j],
                                 start=True, stop=True)
                    last.then_inc(g_mm, 1)
                for j in sorted(beside):
                    beside[j]()

            def sums(i, started, beside, info=None):
                info = info or load_info(nc, pe, body_info, i, N, 4)
                either(pe, [], info[3] < 1, lambda: narrow_body(i, started, beside),
                       lambda: wide_body(i, started, beside))

            def p2_steps(b, warm):
                def kv():
                    pe.wait_ge(s_tl, 16 * b + 16)
                    for s in range(2):
                        u = 2 * b + s
                        if warm:
                            pe.wait_ge(c_v, u - 1)
                        for k in range(K2):
                            M(bank[4 + s][0:U, D:2 * D], xnt[:, s, k], wqkv_s[:, k, 2 * D:3 * D], start=(k == 0),
                              stop=(k == K2 - 1))
                        for k in range(K2):
                            M(bank[4 + s][0:U, 0:D], xnt[:, s, k], wqkv_s[:, k, D:2 * D], start=(k == 0), stop=False)
                        M(bank[4 + s][0:U, 0:D], ones[0:1, 0:U], nkrow[:].rearrange("p k n -> p (k n)"), start=False,
                          stop=True).then_inc(c_kv, 1)

                def context():
                    for s in range(2):
                        u = 2 * b + s
                        pe.wait_ge(c_exp, u + 1)
                        pe.wait_ge(c_v, u + 1)
                        for k in range(K2):
                            M(bank[6 + k][:, 0:D], t1[0:U, s, k * P:(k + 1) * P], t0[0:U, s],
                              start=not warm and s == 0, stop=False, skip_group_check=True)
                            last = M(bank[6 + k][:, D:D + 1], t0[0:U, s, k * P:(k + 1) * P], ones[0:U, 0:1],
                                     start=False, stop=False, skip_group_check=True)
                        last.then_inc(c_ctx, 1)
                return {1: kv, 9: context}
            pe.wait_ge(g_idx, 2)
            repeat(pe, t, lambda i, warm: sums(i, warm, p2_steps(i, warm)), 0, PAIRS)
            for k in range(K2):
                M(bank[6 + k][:, 0:D], zeros[:], b5_s[0:1], start=False, stop=True, skip_group_check=True)
                M(bank[6 + k][:, D:D + 1], zeros[:], ones[0:1, 0:1], start=False, stop=True,
                  skip_group_check=True).then_inc(c_end, 1)
            pe.wait_ge(w_ctx, 1)
            pe.wait_ge(s_constv, 1)
            for k in range(K2):
                last = M(bank[4][:, k * D:k * D + D], ctx_t[:, k], wout_s[:, k], start=True, stop=True)
            last.then_inc(w_mm, 1)
            pe.wait_ge(w_done, K2)

            def p3_steps(b, warm):
                def query():
                    pe.wait_ge(s_tl, 16 * (PAIRS + 1) + 16 * b)
                    for s in range(2):
                        if warm:
                            pe.wait_ge(q_exp, 2 * b + s - 1)
                        for k in range(K2):
                            last = M(bank[2 + s][0:U, 0:D], xnt[:, s, k], wqkv_s[:, k, 0:D], start=(k == 0),
                                     stop=(k == K2 - 1))
                        last.then_inc(q_q, 1)

                def turn_query():
                    for s in range(2):
                        pe.wait_ge(q_norm, 2 * b + s - 1)
                        turn_unit(t0[0:U, s], s, bank[4 + s], 0, q_tr)

                def mix():
                    for s in range(2):
                        pe.wait_ge(q_trc, 2 * b + s - 1)
                        if s == 0 and not (isinstance(b, int) and b == 1):
                            pe.wait_ge(q_ln, 2 * b - 2)
                        for k in range(K2):
                            last = M(bank[6 + s][0:U, 0:D], h1t[:, s, k], mix_w[:, k], start=(k == 0),
                                     stop=(k == K2 - 1))
                        last.then_inc(q_o, 1)
                return {0: query, 2: turn_query, 11: mix} if warm else {0: query}
            sums(PAIRS, True, p3_steps(0, False))
            sums(PAIRS + 1, True, p3_steps(1, True))
            repeat(pe, t, lambda i, warm: sums(i, True, p3_steps(i - PAIRS, True)), PAIRS + 2, 2 * PAIRS)
            last_steps = p3_steps(PAIRS, True)
            sums(2 * PAIRS, True, {0: last_steps[2], 8: last_steps[11]})
            final = FinalUnits(pe, U, UNITS)

            def turn_weights(n):
                pe.wait_ge(f_g, n)
                pe.transpose(bank[2][0:NE + 1, 0:U], g5[0:U, 0], ident[0:U, 0:U]).then_inc(f_gt, 1)

            def spread_weights(n):
                pe.wait_ge(f_gtc, n)
                for q in range(NE // 2):
                    last = M(bank[3][:, q * U:q * U + U], spread[:, q], g5t[0:NE, 0], start=True, stop=True)
                last.then_inc(f_gb, 1)

            def mlp_out(n):
                pe.wait_ge(f_h2, n)
                pe.wait_ge(f_e2g, n)
                M(bank[2][0:U, D:2 * D], h2t[:, 0], sw3_s[:], start=True, stop=False)
                M(bank[2][0:U, D:2 * D], g5t[:, 0], b5_s[:], start=False, stop=False)
                for q in range(NE // 2):
                    last = M(bank[2][0:U, D:2 * D], e2g[:, 0, q], ew3_s[:, q], start=False, stop=(q == 1))
                last.then_inc(f_o, 1)

            def graph_out(n):
                pe.wait_ge(f_ag, n + 1)
                for k in range(K2):
                    last = M(bank[4][0:U, 0:D], xnt[:, 0, k], gnnw_s[:, k], start=(k == 0), stop=(k == K2 - 1))
                last.then_inc(f_y, 1)

            def turn_z(n):
                pe.wait_ge(f_zn, n + 1)
                turn_unit(t0[0:U, 0], 0, bank[4], D, f_tr)

            def first_layers(n):
                pe.wait_ge(f_znt, n + 1)
                for k in range(K2):
                    last = M(bank[3][0:U, D:D + NE], t3t[:, 0, k], gw_s[:, k], start=(k == 0), stop=(k == K2 - 1))
                last.then_inc(f_log, 1)
                for p in range(K2):
                    for k in range(K2):
                        M(bank[5][:, p * U:p * U + U], sw1_s[:, k, p * P:p * P + P], t3t[:, 0, k],
                          start=(k == 0), stop=(k == K2 - 1))
                for e in range(NE):
                    for k in range(K2):
                        last = M(bank[6][:, e * U:e * U + U], ew1_s[:, k, e], t3t[:, 0, k], start=(k == 0),
                                 stop=(k == K2 - 1))
                last.then_inc(f_h, 1)

            def second_layers(n):
                pe.wait_ge(f_relu, n)
                for k in range(K2):
                    M(bank[5][:, D:D + U], sw2_s[:, k], h1t[:, 0, k], start=(k == 0), stop=(k == K2 - 1))
                for e in range(NE):
                    p0 = EH2 * (e % 2)
                    last = M(bank[7][p0:p0 + EH2, (e // 2) * U:(e // 2) * U + U], ew2_s[:, e], e1t[:, 0, e],
                             start=True, stop=True)
                last.then_inc(f_2, 1)

            def after_first(n, step):
                def run():
                    with pe.If(n > 0):
                        step(n)
                return run

            def unit_steps(n):
                return {0: lambda: graph_out(n), 4: after_first(n, turn_weights), 5: after_first(n, second_layers),
                        7: after_first(n, spread_weights), 9: lambda: turn_z(n), 10: after_first(n, mlp_out),
                        RING: lambda: first_layers(n)}

            with pe.Fori(2 * PAIRS + 1, BODIES) as i:
                info = load_info(nc, pe, body_info, i, N, 4)
                with final.due(info):
                    n = final.next()
                    sums(i, True, unit_steps(n), info)
                    final.begin()
                with pe.Else():
                    sums(i, True, {}, info)

            def rest(n):
                steps = unit_steps(n)
                for j in sorted(steps):
                    steps[j]()
                final.begin()
            final.run_left(rest)
            second_layers(UNITS)
            turn_weights(UNITS)
            spread_weights(UNITS)
            mlp_out(UNITS)


_INS = ["x", "src", "dst", "edge_type_11", "L0_gnn_weight", "L0_gnn_bias", "L0_gnn_alpha", "L0_mix_Wqkv",
        "L0_mix_Wout", "L0_mix_gamma", "L0_ffn_sW1", "L0_ffn_sb1", "L0_ffn_sW2", "L0_ffn_sb2", "L0_ffn_sW3",
        "L0_ffn_sb3", "L0_ffn_eW1", "L0_ffn_eb1", "L0_ffn_eW2", "L0_ffn_eb2", "L0_ffn_eW3", "L0_ffn_eb3",
        "L0_ffn_gW", "L0_ffn_gb"]


def kernel(**inputs):
    import numpy as _np
    import concourse.bacc as _bacc
    from concourse import mybir as _mybir
    from concourse.bass_utils import run_bass_kernel_spmd as _run

    nc = _bacc.Bacc("TRN2", target_bir_lowering=False, num_devices=1)
    arrays, args = {}, []
    for name in _INS:
        a = _np.ascontiguousarray(inputs[name])
        arrays[f"in_{name}_dram"] = a
        args.append(nc.dram_tensor(f"in_{name}_dram", a.shape, _mybir.dt.from_np(a.dtype), kind="ExternalInput").ap())
    shape = inputs["x"].shape
    args.append(nc.dram_tensor("out_0_dram", shape, _mybir.dt.float32, kind="ExternalOutput").ap())
    program(nc, *args)
    r = _run(nc, [arrays], core_ids=[0])
    return r.results[0]["out_0_dram"]
```
